# Optimizing a Trainium2 kernel written in Bass

```python
import numpy as np
import jax
import jax.numpy as jnp

def _softmax(x, axis=-1):
    return jax.nn.softmax(x, axis=axis)

def _gelu(x):
    return jax.nn.gelu(x, approximate=True)

def _silu(x):
    return jax.nn.silu(x)

def _sigmoid(x):
    return jax.nn.sigmoid(x)

def _layernorm(x, axis=-1, eps=1e-05):
    m = jnp.mean(x, axis=axis, keepdims=True)
    v = jnp.var(x, axis=axis, keepdims=True)
    return (x - m) / jnp.sqrt(v + eps)

def _scatter_add(tgt, idx, src, axis=0):
    return tgt.at[idx].add(src)

def _segment_sum(src, seg, n):
    return jax.ops.segment_sum(src, seg, n)
kernel_name = 'mk_prb_d1_jaxref_r8_417d11'

def setup_inputs(seed: int=0):
    np.random.seed(seed)
    _w = jnp.asarray

    def _L0_attn_setup():
        import jax, jax.numpy as jnp
        import numpy as np
        D_MODEL = 128
        H = 8
        S = 128
        HD = 128
        LV = 12
        B = 2
        T = 256

        def _level_structure(t, num_levels):
            idx = np.arange(t)
            d = idx[:, None] - idx[None, :]
            lvl = np.where(d <= 0, 0, np.floor(np.log2(np.maximum(d, 1))).astype(np.int64) + 1)
            lvl = np.minimum(lvl, num_levels - 1)
            mask = d >= 0
            return (jnp.asarray(lvl), jnp.asarray(mask))
        key = jax.random.key(seed)
        ks = jax.random.split(key, 8)
        sd = 1.0 / np.sqrt(D_MODEL)
        return {'x': jax.random.normal(ks[0], (B, T, D_MODEL), jnp.float32), 'Wq': jax.random.normal(ks[1], (H * S, D_MODEL), jnp.float32) * sd, 'Wk': jax.random.normal(ks[2], (H * S, D_MODEL), jnp.float32) * sd, 'Wv': jax.random.normal(ks[3], (H * HD, D_MODEL), jnp.float32) * sd, 'Wg': jax.random.normal(ks[4], (H, D_MODEL), jnp.float32) * sd, 'bg': jnp.zeros((H,), jnp.float32), 'Wdl': jax.random.normal(ks[5], (H * LV, D_MODEL), jnp.float32) * sd, 'Lparam': jnp.ones((H, LV), jnp.float32), 'Wo': jax.random.normal(ks[6], (D_MODEL, H * HD), jnp.float32) / np.sqrt(H * HD), 'ln_g': jnp.ones((D_MODEL,), jnp.float32), 'ln_b': jnp.zeros((D_MODEL,), jnp.float32)}
    _L0_attn_in = _L0_attn_setup()

    def _L0_ffn_setup():
        import jax, jax.numpy as jnp
        import numpy as np
        B, T, D, F, E = (2, 128, 128, 512, 8)
        EPS = 1e-06
        key = jax.random.key(seed)
        k = jax.random.split(key, 5)
        scale = 0.02
        return {'x': jax.random.normal(k[0], (B, T, D), dtype=jnp.float32), 'rms_w': jnp.ones((D,), dtype=jnp.float32), 'gate_w': jax.random.normal(k[1], (E, D), dtype=jnp.float32) * scale, 'W1': jax.random.normal(k[2], (E, D, F), dtype=jnp.float32) * scale, 'b1': jnp.zeros((E, F), dtype=jnp.float32), 'W2': jax.random.normal(k[3], (E, F, D), dtype=jnp.float32) * scale, 'b2': jnp.zeros((E, D), dtype=jnp.float32)}
    _L0_ffn_in = _L0_ffn_setup()
    _d = {'L0_attn_x': _L0_attn_in['x'], 'L0_attn_Wq': _L0_attn_in['Wq'], 'L0_attn_Wk': _L0_attn_in['Wk'], 'L0_attn_Wv': _L0_attn_in['Wv'], 'L0_attn_Wg': _L0_attn_in['Wg'], 'L0_attn_bg': _L0_attn_in['bg'], 'L0_attn_Wdl': _L0_attn_in['Wdl'], 'L0_attn_Lparam': _L0_attn_in['Lparam'], 'L0_attn_Wo': _L0_attn_in['Wo'], 'L0_attn_ln_g': _L0_attn_in['ln_g'], 'L0_attn_ln_b': _L0_attn_in['ln_b'], 'L0_ffn_rms_w': _L0_ffn_in['rms_w'], 'L0_ffn_gate_w': _L0_ffn_in['gate_w'], 'L0_ffn_W1': _L0_ffn_in['W1'], 'L0_ffn_b1': _L0_ffn_in['b1'], 'L0_ffn_W2': _L0_ffn_in['W2'], 'L0_ffn_b2': _L0_ffn_in['b2']}
    _x0 = _d['L0_attn_x']
    _d['L0_attn_x'] = jax.random.normal(jax.random.fold_in(jax.random.key(seed), 1), (32, 256, 128), dtype=_x0.dtype)
    del _x0
    return _d

def reference(L0_attn_x, L0_attn_Wq, L0_attn_Wk, L0_attn_Wv, L0_attn_Wg, L0_attn_bg, L0_attn_Wdl, L0_attn_Lparam, L0_attn_Wo, L0_attn_ln_g, L0_attn_ln_b, L0_ffn_rms_w, L0_ffn_gate_w, L0_ffn_W1, L0_ffn_b1, L0_ffn_W2, L0_ffn_b2):

    def _L0_attn_ref(x, Wq, Wk, Wv, Wg, bg, Wdl, Lparam, Wo, ln_g, ln_b):
        import jax, jax.numpy as jnp
        import numpy as np
        D_MODEL = 128
        H = 8
        S = 128
        HD = 128
        LV = 12
        B = 2
        T = 256

        def _level_structure(t, num_levels):
            idx = np.arange(t)
            d = idx[:, None] - idx[None, :]
            lvl = np.where(d <= 0, 0, np.floor(np.log2(np.maximum(d, 1))).astype(np.int64) + 1)
            lvl = np.minimum(lvl, num_levels - 1)
            mask = d >= 0
            return (jnp.asarray(lvl), jnp.asarray(mask))
        b, t, _ = x.shape
        q = (x @ Wq.T).reshape(b, t, H, S)
        k = (x @ Wk.T).reshape(b, t, H, S)
        v = (x @ Wv.T).reshape(b, t, H, HD)
        g = -jax.nn.softplus(x @ Wg.T + bg)
        dl = (x @ Wdl.T).reshape(b, t, H, LV)
        lam = jax.nn.softplus(dl + Lparam[None, None])
        G = jnp.cumsum(g, axis=1)
        lvl, mask = _level_structure(t, LV)
        scale = 1.0 / np.sqrt(S)
        scores = jnp.einsum('bthd,bshd->bhts', q, k) * scale
        Gh = G.transpose(0, 2, 1)
        logdecay = Gh[:, :, :, None] - Gh[:, :, None, :]
        logdecay = jnp.where(mask[None, None], logdecay, -jnp.inf)
        decay = jnp.exp(logdecay)
        lvl_oh = jax.nn.one_hot(lvl, LV, dtype=x.dtype)
        lamw = jnp.einsum('bthl,tsl->bhts', lam, lvl_oh)
        A = scores * decay * lamw
        y = jnp.einsum('bhts,bshd->bthd', A, v).reshape(b, t, H * HD)
        out = y @ Wo.T + x
        mu = out.mean(-1, keepdims=True)
        var = out.var(-1, keepdims=True)
        return (out - mu) * jax.lax.rsqrt(var + 1e-05) * ln_g + ln_b

    def _L0_ffn_ref(x, rms_w, gate_w, W1, b1, W2, b2):
        import jax, jax.numpy as jnp
        import numpy as np
        B, T, D, F, E = (2, 128, 128, 512, 8)
        EPS = 1e-06
        ms = jnp.mean(x * x, axis=-1, keepdims=True)
        xn = x * jax.lax.rsqrt(ms + EPS) * rms_w
        logits = jnp.einsum('btd,ed->bte', xn, gate_w)
        scores = jax.nn.softmax(logits, axis=-1)
        top1_idx = jnp.argmax(scores, axis=-1)
        top1_score = jnp.max(scores, axis=-1)
        out = jnp.zeros_like(xn)
        for e in range(E):
            h = jax.nn.silu(jnp.einsum('btd,df->btf', xn, W1[e]) + b1[e])
            ye = jnp.einsum('btf,fd->btd', h, W2[e]) + b2[e]
            out = jnp.where((top1_idx == e)[..., None], ye, out)
        return out * top1_score[..., None]
    x = L0_attn_x
    xn = _layernorm(x, axis=-1)
    x = x + _L0_attn_ref(xn, L0_attn_Wq, L0_attn_Wk, L0_attn_Wv, L0_attn_Wg, L0_attn_bg, L0_attn_Wdl, L0_attn_Lparam, L0_attn_Wo, L0_attn_ln_g, L0_attn_ln_b) + _L0_ffn_ref(xn, L0_ffn_rms_w, L0_ffn_gate_w, L0_ffn_W1, L0_ffn_b1, L0_ffn_W2, L0_ffn_b2)
    return x

_drawn_inputs = setup_inputs


def setup_inputs(seed=0):
    import zlib

    import numpy as np

    out = dict(_drawn_inputs(seed))
    spreads = {'L0_attn_bg': (0.0, 0.8),
     'L0_attn_Lparam': (1.0, 0.6),
     'L0_attn_ln_g': (1.0, 0.2),
     'L0_attn_ln_b': (0.0, 0.317),
     'L0_ffn_rms_w': (1.0, 0.6),
     'L0_ffn_b1': (0.0, 0.8),
     'L0_ffn_b2': (0.0, 0.8)}
    factors = {'L0_ffn_gate_w': 5.25, 'L0_ffn_W1': 8.0, 'L0_ffn_W2': 8.0}
    for name, (base, spread) in spreads.items():
        noise = np.random.default_rng([zlib.crc32(name.encode()), seed]).standard_normal(out[name].shape)
        drawn = base * np.exp(spread * noise) if base else spread * noise
        out[name] = jnp.asarray(drawn.astype(out[name].dtype))
    for name, factor in factors.items():
        out[name] = (out[name] * factor).astype(out[name].dtype)
    return out
```

```python
from contextlib import ExitStack

import concourse.bass as bass
import numpy as np
from concourse import mybir

ALU = mybir.AluOpType
ACT = mybir.ActivationFunctionType
F32 = mybir.dt.float32
BF16 = mybir.dt.bfloat16
U16 = mybir.dt.uint16
AX_X = mybir.AxisListType.X

P = 128
NB, T, D = 32, 256, 128
H = 8
LV = 9
TW = 4
NP3 = 3
HG = 4
VR = NP3 * TW * LV
CR = NP3 * HG * LV
KR = VR + TW
LW = T - TW + P
NT = NB * T // P
E, F = 8, 512
FT = F // P
BIG = -1.0e30
LAM_MIN = 2.0 ** -63
UNITS = [(0, 0), (0, 1), (1, 1)]
ROUNDS = 16
R_T, R_DL, R_GATE, R_Z, R_U, R_GT, R_V = 0, 1, 2, 3, 7, 11, 12
HALF = NB // 2
XW = D + 4
C_RMS, C_SCORE = D, D + 1
ST = NT + E
GRP = 4
NG = NT // GRP
NS = 4


def bf16_bits(a):
    return (np.ascontiguousarray(a, np.float32).view(np.uint32) >> 16).astype(np.uint16)


def level_constants():
    d = np.arange(TW)[:, None] - (np.arange(LW)[None, :] - (T - TW))
    lvl = np.where(d <= 0, 0, np.floor(np.log2(np.maximum(d, 1))).astype(int) + 1)
    m = np.zeros((KR, LW), np.float32)
    for p in range(NP3):
        for q in range(TW):
            for l in range(LV):
                m[(p * TW + q) * LV + l] = (d[q] >= 0) & (lvl[q] == l)
    m[VR:] = d < 0
    own = np.zeros((VR, T), np.float32)
    for r in range(VR):
        own[r] = np.arange(T) % TW == (r // LV) % TW
    causal = np.zeros((TW, H, T), np.float32)
    for q in range(TW):
        causal[q, :, q::TW] = BIG
    rep = np.zeros((CR, HG, VR), np.float32)
    for p in range(NP3):
        for h in range(HG):
            for q in range(TW):
                for l in range(LV):
                    rep[(p * HG + h) * LV + l, h, (p * TW + q) * LV + l] = 1
    part = np.arange(CR) // (HG * LV)
    minus = np.stack([-(part >= 1).astype(np.float32), -(part >= 2).astype(np.float32)], 1)
    return {
        "c_level": bf16_bits(m), "c_own": own, "c_causal": bf16_bits(causal.reshape(TW, H * T)),
        "c_before": bf16_bits(np.triu(np.ones((P, P), np.float32), 1)), "c_all": bf16_bits(np.ones((P, P), np.float32)),
        "c_eid": np.tile(np.arange(E, dtype=np.float32), (P, 1)), "c_kP": np.tile(P * np.arange(NT, dtype=np.float32), (P, 1)),
        "c_tile": np.tile(np.arange(ST, dtype=np.float32), (P, 1)),
        "c_prow": np.stack([np.arange(NP3 * E) % E, -1.0 * (np.arange(NP3 * E) >= E), -1.0 * (np.arange(NP3 * E) >= 2 * E)], 1).astype(np.float32),
        "c_rep": bf16_bits(rep.reshape(CR, HG * VR)), "c_minus": minus, "c_ident": np.eye(P, dtype=np.float32),
    }


def build(nc, a, out):
    ctx = ExitStack()
    with ctx:
        def sb(name, shape, dt=F32):
            return ctx.enter_context(nc.sbuf_tensor(name, shape, dt))

        def psum(name, shape):
            return ctx.enter_context(nc.psum_tensor(name, shape, F32))

        def sem(name):
            return ctx.enter_context(nc.semaphore(name))

        level = sb("level", [KR, LW], BF16)
        own = sb("own", [VR, T])
        rep = sb("rep", [CR, HG, VR], BF16)
        minus = sb("minus", [CR, 2])
        ident = sb("ident", [P, P])
        wdl = sb("wdl", [P, 2, CR])
        wg = sb("wg", [P, 2, CR])
        zbias = sb("zbias", [CR, 4])
        lng = sb("lng", [P, D])
        lnb = sb("lnb", [P, D])
        wstage = sb("wstage", [P, 4, H * D])
        w1 = wstage[:].rearrange("p a b -> p (a b)").rearrange("p (e f) -> p e f", e=E)
        w2 = sb("w2", [P, E, FT, D])
        gate = sb("gate", [P, E])
        rmsw = sb("rmsw", [P, 1])
        before = sb("before", [P, P], BF16)
        allones = sb("allones", [P, P], BF16)
        eid = sb("eid", [P, E])
        kP = sb("kP", [P, NT])
        tileid = sb("tileid", [P, ST])
        prow = sb("prow", [NP3 * E, 3])
        bparts = sb("bparts", [NP3 * E, F + D], BF16)
        slot = sb("slot", [P, NT], mybir.dt.uint32)
        texp = sb("texp", [P, ST])
        texpi = sb("texpi", [1, ST], mybir.dt.int32)
        tsel = sb("tsel", [NP3 * E, ST])
        ssq = sb("ssq", [P, NT])
        idle0 = sb("idle0", [1, 1])
        idle = sb("idle", [1, 1])
        rowst = sb("rowst", [P, 4, XW])
        slotst = sb("slotst", [P, 4], mybir.dt.uint32)
        got = sb("got", [P, 4, D])
        ones128 = sb("ones128", [P, P])
        small64 = sb("small64", [P, 2, NT])
        small = sb("small", [P, 8, E])
        m_all = sb("m_all", [P, H, D])
        n_all = sb("n_all", [P, H * D])
        x_all = sb("x_all", [P, NT, D])
        xn_all = sb("xn_all", [P, NT, XW])
        stats = sb("stats", [P, NT, 6])
        msum = sb("msum", [P, NT, 2])
        mdif = sb("mdif", [P, NT])
        mean = sb("mean", [P, NT])
        dev = sb("dev", [P, NT])
        rstd = sb("rstd", [P, NT])
        lnv = sb("lnv", [P, NT])
        junk = sb("junk", [P, D])
        xnb = sb("xnb", [P, 2, D])
        xnT = sb("xnT", [P, 2, T])
        zT = sb("zT", [P, 2, H, T])
        u = sb("u", [P, 2, 2, H * D])
        val = sb("val", [KR, 2, H, T], BF16)
        negG = sb("negG", [P, 2, 4, HG])
        zz = sb("zz", [CR, 4, T])
        na = sb("na", [CR, 4, T])
        ones = sb("ones", [CR, T])
        gsum = sb("gsum", [CR, 2, T])
        lnlam = sb("lnlam", [CR, 2, T])
        v32 = sb("v32", [CR, 2, T])
        vb = sb("vb", [CR, 2, T], BF16)
        vparts = sb("vparts", [CR, 2, T], BF16)
        expo = sb("expo", [P, 2, H, P])
        att = sb("att", [P, 2, H, P])
        o = sb("o", [P, 2, D])
        ostats = sb("ostats", [P, 2, 6])
        osum = sb("osum", [P, 2, 2])
        odif = sb("odif", [P, 2])
        omean = sb("omean", [P, 2])
        odev = sb("odev", [P, 2])
        orstd = sb("orstd", [P, 2])
        y = sb("y", [P, 2, D])

        epsc = sb("epsc", [P, 4])
        stage = [expo[:, k].rearrange("p h t -> p (h t)")[:, 0:GRP * P].rearrange("p (a d) -> p a d", a=GRP) for k in range(2)]
        stageT = [att[:, k].rearrange("p h t -> p (h t)")[:, 0:GRP * P] for k in range(2)]
        zflat = zT[:].rearrange("p k h t -> p (k h t)")
        uflat = u[:].rearrange("p k n d -> p (k n d)")
        grid = [uflat[:, 512 * k:512 * k + 512] for k in range(8)]
        tgrid = zflat[:, 0:ST * E]
        onehot = zflat[:, 1024:1024 + NT * E // 2].bitcast(BF16)
        zfree = zT[:, 1].rearrange("p h t -> p (h t)")
        ufree = u[:, 1].rearrange("p n d -> p (n d)")
        bias32 = na[0:NP3 * E].rearrange("p a t -> p (a t)")[:, 0:F + D]
        biasr = zz[0:NP3 * E].rearrange("p a t -> p (a t)")[:, 0:F + D]
        xs = zfree[:, 0:NS * XW].rearrange("p (k d) -> p k d", k=NS)
        xf = zfree[:, 528:528 + 2 * D].rearrange("p (k d) -> p k d", k=2)
        xfT = zfree[:, 784:784 + 2 * D].rearrange("p (k d) -> p k d", k=2)
        yb = got
        sel = zfree[0:NP3 * E, 1552:1552 + NS * D // 2].bitcast(BF16).rearrange("p (k d) -> p k d", k=NS)
        hb = ufree[:, 0:2 * F].rearrange("p (k f) -> p k f", k=2)
        hT = ufree[:, 2 * F:4 * F].rearrange("p (k f) -> p k f", k=2)

        misc = psum("misc", [P, 2, 512])
        arg = psum("arg", [P, 2, H, 64])
        sc = psum("sc", [P, 2, 4, P])
        acc = psum("acc", [P, 2, 512])

        arg_bank = [arg[:, k].rearrange("p h t -> p (h t)") for k in range(2)]

        def staggered(stages, eng):
            low, high = -3, ST + 1
            start, end = NS, (ST - NS) // NS * NS

            def step(k, q, static):
                for off, stage_ in stages:
                    if not static or 0 <= k + off < ST:
                        stage_(k + off, (q + off) % NS)

            for k in range(low, start):
                step(k, k % NS, True)
            with eng.Fori(start // NS, end // NS) as i:
                for q in range(NS):
                    step(NS * i + q, q, False)
            for k in range(end, high):
                step(k, k % NS, True)

        loads = sem("loads")
        wloads = sem("wloads")
        xload = [sem(f"xload{c}") for c in range(4)]
        stat_step = sem("stat_step")
        stats_step = sem("stats_step")
        omom_step = sem("omom_step")
        stats_done = sem("stats_done")
        rstd_step = sem("rstd_step")
        rstd_done = sem("rstd_done")
        xn_done = sem("xn_done")
        mn_full = sem("mn_full")
        mn_used = sem("mn_used")
        const_set = sem("const_set")
        xnb_done = sem("xnb_done")
        misc_full = sem("misc_full")
        act_misc = sem("act_misc")
        dve_misc = sem("dve_misc")
        zz_done = sem("zz_done")
        na_done = sem("na_done")
        ex_done = sem("ex_done")
        l1_done = sem("l1_done")
        sp_done = sem("sp_done")
        lnlam_done = sem("lnlam_done")
        scan_done = sem("scan_done")
        part_step = sem("part_step")
        parts_done = sem("parts_done")
        arg_full = sem("arg_full")
        exp_done = sem("exp_done")
        s_full = sem("s_full")
        mult_done = sem("mult_done")
        av_done = sem("av_done")
        ln_step = sem("ln_step")
        ostat_done = sem("ostat_done")
        olog_done = sem("olog_done")
        orstd_done = sem("orstd_done")
        y_done = sem("y_done")
        y_step = sem("y_step")
        stored = sem("stored")
        w1_loaded = sem("w1_loaded")
        w1_ready = sem("w1_ready")
        gate_ready = sem("gate_ready")
        bias_step = sem("bias_step")
        staged = sem("staged")
        turned = sem("turned")
        unturned = sem("unturned")
        ssq_done = sem("ssq_done")
        rr_step = sem("rr_step")
        rr_done = sem("rr_done")
        logit_full = sem("logit_full")
        sort_step = sem("sort_step")
        score_exp = sem("score_exp")
        onehot_done = sem("onehot_done")
        rank_full = sem("rank_full")
        sorted_ = sem("sorted_")
        zero_set = sem("zero_set")
        zeroed = sem("zeroed")
        row_copy = sem("row_copy")
        row_out = [sem(f"row_out{q}") for q in range(4)]
        xs_in = [sem(f"xs_in{q}") for q in range(NS)]
        xf_done = sem("xf_done")
        sel_done = sem("sel_done")
        xT_full = sem("xT_full")
        xT_done = sem("xT_done")
        h_full = sem("h_full")
        h_done = sem("h_done")
        hT_full = sem("hT_full")
        hT_done = sem("hT_done")
        yx_full = sem("yx_full")
        yx_done = sem("yx_done")
        y_out = [sem(f"y_out{q}") for q in range(NS)]
        slot_copy = sem("slot_copy")
        got_in = [sem(f"got_in{q}") for q in range(4)]
        got_scored = sem("got_scored")
        got_added = sem("got_added")

        x_dram = a["x"].rearrange("(n p) d -> p n d", p=P)
        out_dram = out.rearrange("(n p) d -> p n d", p=P)
        XC = NT // 4
        rows_dram = nc.dram_tensor("rows_by_slot", (ST * P, XW), F32, kind="Internal").ap()
        y_dram = nc.dram_tensor("y_by_slot", (ST * P, D), F32, kind="Internal").ap()
        rows_tiles = rows_dram.rearrange("(n p) d -> p n d", p=P)
        y_tiles = y_dram.rearrange("(n p) d -> p n d", p=P)

        block = ctx.enter_context(nc.Block())

        ACT_ROUNDS = [R_T] + [R_Z + k for k in range(4)] + [R_U + k for k in range(4)]
        DVE_ROUNDS = [R_DL, R_GATE, R_GT] + [R_V + k for k in range(4)]

        def emptied(eng, b, r, first):
            if r >= 2:
                prev, back = r - 2, 0
            elif first:
                return
            else:
                prev, back = r - 2 + ROUNDS, 1
            if prev in ACT_ROUNDS:
                eng.wait_ge(act_misc, b * len(ACT_ROUNDS) + (ACT_ROUNDS.index(prev) + 1 - back * len(ACT_ROUNDS)))
            else:
                eng.wait_ge(dve_misc, b * len(DVE_ROUNDS) + (DVE_ROUNDS.index(prev) + 1 - back * len(DVE_ROUNDS)))

        def sequences(body, last=None):
            raise NotImplementedError

        @block.sync
        def _(sp):
            for c in range(4):
                sp.dma_start(x_all[:, c * XC:(c + 1) * XC, :], x_dram[:, c * XC:(c + 1) * XC, :]).then_inc(xload[c], 16)
            for dst, name in ((ident, "c_ident"), (own, "c_own"), (minus, "c_minus"), (zbias, "zbias"), (lng, "lng"), (lnb, "lnb"),
                              (gate, "gate"), (rmsw, "rmsw"), (eid, "c_eid"), (kP, "c_kP"), (tileid, "c_tile"), (prow, "c_prow"), (bias32, "bias")):
                sp.dma_start(dst[:], a[name]).then_inc(loads, 16)
            sp.dma_start(wdl[:].rearrange("p g c -> p (g c)"), a["wdl"]).then_inc(loads, 16)
            sp.dma_start(wg[:].rearrange("p g c -> p (g c)"), a["wg"]).then_inc(loads, 16)
            sp.dma_start(level[:], a["c_level"].bitcast(BF16)).then_inc(loads, 16)
            sp.dma_start(rep[:].rearrange("p h v -> p (h v)"), a["c_rep"].bitcast(BF16)).then_inc(loads, 16)
            for k in range(2):
                sp.dma_start(val[VR:KR, k].rearrange("p h t -> p (h t)"), a["c_causal"].bitcast(BF16)).then_inc(loads, 16)
            for dst, name in ((before, "c_before"), (allones, "c_all")):
                sp.dma_start(dst[:], a[name].bitcast(BF16)).then_inc(loads, 16)
            for k in range(4):
                sp.dma_start(wstage[:, k, :], a["w4"][k]).then_inc(wloads, 16)
            sp.wait_ge(mn_full, 4)
            sp.dma_start(wstage[:].rearrange("p a b -> p (a b)"), a["w1"]).then_inc(w1_loaded, 16)
            sp.dma_start(w2[:].rearrange("p e t d -> p (e t d)"), a["w2"]).then_inc(w1_loaded, 16)
            sp.wait_ge(zero_set, 1)
            sp.dma_start(rows_tiles, rowst[:, 0:1, :].broadcast_to([P, ST, XW])).then_inc(zeroed, 16)

            for q in range(4):
                sp.wait_ge(row_out[q], 16 * HALF)
            sp.wait_ge(av_done, 3 * HALF)
            for q in range(NS):
                sp.dma_start(xs[:, q, :], rows_tiles[:, q, :]).then_inc(xs_in[q], 16)

            for q in range(NS):
                sp.wait_ge(xf_done, q + 1)
                sp.dma_start(xs[:, q, :], rows_tiles[:, NS + q, :]).then_inc(xs_in[q], 16)

            def exchange(k, q, last):
                sp.wait_ge(yx_done, k + 1)
                sp.dma_start(y_tiles[:, bass.ds(k, 1), :], yb[:, q:q + 1, :]).then_inc(y_out[q], 16)
                if not last:
                    sp.wait_ge(xf_done, k + (NS + 1))
                    sp.dma_start(xs[:, q:q + 1, :], rows_tiles[:, bass.ds(k + 2 * NS, 1), :]).then_inc(xs_in[q], 16)

            with sp.Fori(0, ST // NS - 2) as i:
                for q in range(NS):
                    exchange(NS * i + q, q, False)
            for k in range(ST - 2 * NS, ST):
                exchange(k, k % NS, True)

            with sp.Fori(0, HALF - 1) as i:
                sp.wait_ge(got_added, 4 * i + 4)
                sp.dma_start(out_dram[:, bass.ds(4 * i, 4), :], x_all[:, bass.ds(4 * i, 4), :]).then_inc(stored, 16)
            sp.wait_ge(y_step, 3 * NB)
            sp.dma_start(out_dram[:, NT - 4:NT, :], x_all[:, NT - 4:NT, :]).then_inc(stored, 16)
            sp.wait_ge(stored, 16 * HALF)
        LOADS = 21 * 16

        @block.tensor
        def _(pe):
            def mn_products():
                pe.wait_ge(wloads, 64)
                for k in range(4):
                    src = 2 * (k // 2)
                    for q in range(4):
                        h = 4 * (k % 2) + q
                        dst = (sc[:, k % 2] if k < 2 else acc[:, k % 2].rearrange("p (h d) -> p h d", d=D))[:, q]
                        mm = nc.tensor.matmul(dst, wstage[:, src, h * D:(h + 1) * D], wstage[:, src + 1, h * D:(h + 1) * D],
                                              start=True, stop=True)
                    mm.then_inc(mn_full, 1)

            def r_turn(b, k, first):
                pe.wait_ge(xnb_done, b * 1 + 1)
                emptied(pe, b, R_T, first)
                for n in range(2):
                    mm = nc.tensor.transpose(misc[:, R_T % 2, n * P:(n + 1) * P], xnb[:, n], ident[:])
                mm.then_inc(misc_full, 1)

            def r_values(b, k, first):
                pe.wait_ge(act_misc, b * len(ACT_ROUNDS) + 1)
                for r, w in ((R_DL, wdl), (R_GATE, wg)):
                    emptied(pe, b, r, first)
                    for g in range(2):
                        mm = nc.tensor.matmul(misc[0:CR, r % 2, g * T:(g + 1) * T], w[:, g, :], xnT[:, k, :], start=True, stop=True)
                    mm.then_inc(misc_full, 1)

            def r_z(b, k, first):
                for r in range(4):
                    emptied(pe, b, R_Z + r, first)
                    for q in range(2):
                        mm = nc.tensor.matmul(misc[:, (R_Z + r) % 2, q * T:(q + 1) * T], m_all[:, 2 * r + q, :], xnT[:, k, :],
                                              start=True, stop=True)
                    mm.then_inc(misc_full, 1)

            def r_u(b, k, first):
                for r in range(4):
                    emptied(pe, b, R_U + r, first)
                    n, half = r // 2, r % 2
                    nc.tensor.matmul(misc[:, (R_U + r) % 2, :], xnT[:, k, n * P:(n + 1) * P], n_all[:, half * 512:(half + 1) * 512],
                                     start=True, stop=True).then_inc(misc_full, 1)

            def r_gt(b, k, first):
                pe.wait_ge(scan_done, 2 * b + 2)
                emptied(pe, b, R_GT, first)
                for n in range(2):
                    for g in range(2):
                        c = (2 * n + g) * CR
                        mm = nc.tensor.transpose(misc[:, R_GT % 2, c:c + CR], gsum[:, g, n * P:(n + 1) * P], ident[0:CR, 0:CR])
                mm.then_inc(misc_full, 1)

            def r_v(b, k, first, part=range(4)):
                pe.wait_ge(parts_done, b + 1)
                for r in part:
                    emptied(pe, b, R_V + r, first)
                    for q in range(2):
                        h = 2 * r + q
                        mm = nc.tensor.matmul(misc[0:VR, (R_V + r) % 2, q * T:(q + 1) * T], rep[:, h % HG, :], vparts[:, h // HG, :],
                                              start=True, stop=True)
                    mm.then_inc(misc_full, 1)

            def arguments(b, k, n, first):
                ks, qt = UNITS[n]
                if n == 0:
                    pe.wait_ge(dve_misc, b * len(DVE_ROUNDS) + len(DVE_ROUNDS))
                if not (first and n == 0):
                    pe.wait_ge(exp_done, 3 * b + n)
                for j in range(P // TW):
                    t = qt * P + j * TW
                    w = T - TW - (t - ks * P)
                    mm = nc.tensor.matmul(arg[:, j // 16, :, (j % 16) * TW:(j % 16 + 1) * TW], level[:, w:w + P],
                                          val[:, k, :, t:t + TW], start=(j % 16 == 0), stop=True, skip_group_check=True)
                mm.then_inc(arg_full, 1)

            def scores(b, k, n, first):
                ks, qt = UNITS[n]
                if n == 0:
                    pe.wait_ge(act_misc, b * len(ACT_ROUNDS) + len(ACT_ROUNDS))
                for half in range(2):
                    if not (first and n == 0):
                        pe.wait_ge(mult_done, 6 * b + (2 * n + half - 1))
                    nc.tensor.matmul(sc[:, half], xnT[:, k, ks * P:(ks + 1) * P], zT[:, k, 4 * half:4 * half + 4, qt * P:(qt + 1) * P],
                                     start=True, stop=True).then_inc(s_full, 1)

            def weigh(b, k, n, first):
                ks, qt = UNITS[n]
                m = (3 * k + n) % 2
                if n == 0 and not first:
                    pe.wait_ge(ln_step, 4 * b - 3)
                for h in range(H):
                    if h % 4 == 0:
                        pe.wait_ge(mult_done, 6 * b + (2 * n + h // 4 + 1))
                    mm = nc.tensor.matmul(acc[:, qt, 0:D], att[:, m, h, :], u[:, k, ks, h * D:(h + 1) * D],
                                          start=(h == 0 and n < 2), stop=(h == H - 1 and n != 1))
                mm.then_inc(av_done, 1)

            def body(b, k, nxt, first=False):
                c, kn = b + 1, 1 - k
                if nxt:
                    r_turn(c, kn, False)
                arguments(b, k, 0, first)
                scores(b, k, 0, first)
                if nxt:
                    r_values(c, kn, False)
                arguments(b, k, 1, first)
                scores(b, k, 1, first)
                if nxt:
                    r_z(c, kn, False)
                weigh(b, k, 0, first)
                arguments(b, k, 2, first)
                scores(b, k, 2, first)
                if nxt:
                    r_u(c, kn, False)
                if nxt:
                    r_gt(c, kn, False)
                    r_v(c, kn, False, range(2))
                weigh(b, k, 1, first)
                if nxt:
                    r_v(c, kn, False, range(2, 4))
                weigh(b, k, 2, first)

            def router():
                def turn_group(j, k):
                    pe.wait_ge(staged, j + 1)
                    for n in range(GRP):
                        mm = nc.tensor.transpose(arg_bank[k][:, n * P:(n + 1) * P], stage[k][:, n, :], ident[:])
                    mm.then_inc(turned, 1)

                def logit_group(j, k):
                    pe.wait_ge(unturned, j + 1)
                    for n in range(GRP):
                        mm = nc.tensor.matmul(misc[:, 0, bass.ds((j * GRP + n) * E, E)], stageT[k][:, n * P:(n + 1) * P], gate[:],
                                              start=True, stop=True, skip_group_check=True)
                    mm.then_inc(logit_full, 1)

                pe.wait_ge(gate_ready, 1)
                turn_group(0, 0)
                with pe.Fori(0, NG // 2 - 1) as i:
                    turn_group(2 * i + 1, 1)
                    logit_group(2 * i, 0)
                    turn_group(2 * i + 2, 0)
                    logit_group(2 * i + 1, 1)
                turn_group(NG - 1, 1)
                logit_group(NG - 2, 0)
                logit_group(NG - 1, 1)

            def ranks():
                pe.wait_ge(onehot_done, 1)
                nc.tensor.matmul(arg_bank[0], before[:], onehot, start=True, stop=True)
                nc.tensor.matmul(arg_bank[1], allones[:], onehot, start=True, stop=True).then_inc(rank_full, 1)

            def experts():
                def expert_of(n, k):
                    return nc.tensor.value_load(texpi[0:1, bass.ds(k, 1)], min_val=0, max_val=E - 1)

                def turn_rows(k, q):
                    pe.wait_ge(xf_done, k + 1)
                    nc.tensor.transpose(sc[:, q % 2, 0, :], xf[:, q % 2, :], ident[:]).then_inc(xT_full, 1)

                def hidden(k, q):
                    e = expert_of(0, k)
                    pe.wait_ge(xT_done, k + 1)
                    pe.wait_ge(sel_done, k + 1)
                    nc.tensor.matmul(arg_bank[q % 2], sel[:, q, :], bparts[:, 0:F], start=True, stop=False)
                    nc.tensor.matmul(arg_bank[q % 2], xfT[:, q % 2, :], w1[:, bass.ds(e, 1), :].rearrange("p a f -> p (a f)"),
                                     start=False, stop=True).then_inc(h_full, 1)

                def turn_hidden(k, q):
                    pe.wait_ge(h_done, k + 1)
                    for t in range(FT):
                        mm = nc.tensor.transpose(misc[:, q % 2, t * P:(t + 1) * P], hb[:, q % 2, t * P:(t + 1) * P], ident[:])
                    mm.then_inc(hT_full, 1)

                def project(k, q):
                    e = expert_of(1, k)
                    pe.wait_ge(hT_done, k + 1)
                    if not (isinstance(k, int) and k < 2):
                        pe.wait_ge(yx_done, k - 1)
                    nc.tensor.matmul(acc[:, q % 2, D:2 * D], sel[:, q, :], bparts[:, F:F + D], start=True, stop=False)
                    for t in range(FT):
                        mm = nc.tensor.matmul(acc[:, q % 2, D:2 * D], hT[:, q % 2, t * P:(t + 1) * P],
                                              w2[:, bass.ds(e, 1), t, :].rearrange("p a d -> p (a d)"), start=False, stop=(t == FT - 1))
                    mm.then_inc(yx_full, 1)

                pe.wait_ge(w1_ready, 1)
                pe.wait_ge(w1_loaded, 32)
                pe.wait_ge(act_misc, len(ACT_ROUNDS) * (HALF + 1))
                pe.wait_ge(dve_misc, len(DVE_ROUNDS) * (HALF + 1))
                pe.wait_ge(mult_done, 6 * HALF)
                staggered(((2, turn_rows), (1, hidden), (0, turn_hidden), (-1, project)), pe)
                pe.wait_ge(yx_done, ST)

            mn_products()
            pe.wait_ge(loads, LOADS)
            pe.wait_ge(mn_used, 4)
            router()
            ranks()
            pe.wait_ge(sorted_, 1)
            r_turn(0, 0, True)
            r_values(0, 0, True)
            for step in (r_z, r_u, r_gt, r_v):
                step(0, 0, True)
            body(0, 0, True, True)
            body(1, 1, True)
            with pe.Fori(1, HALF // 2) as i:
                body(2 * i, 0, True)
                body(2 * i + 1, 1, True)
            experts()
            with pe.Fori(HALF // 2, NB // 2 - 1) as i:
                body(2 * i, 0, True)
                body(2 * i + 1, 1, True)
            body(NB - 2, 0, True)
            body(NB - 1, 1, False)

        @block.scalar
        def _(act):
            nc.scalar.preload_act_table_set("natural_log_exp_and_others")
            act.wait_ge(const_set, 8)
            act.wait_ge(stats_done, 1)
            nc.scalar.activation(lnv[:], dev[:], ACT.Ln, bias=epsc[:, 0:1], scale=1.0 / D).then_inc(rstd_step, 1)
            act.wait_ge(rstd_step, 1)
            nc.scalar.activation(rstd[:], lnv[:], ACT.Exp, scale=-0.5).then_inc(rstd_done, 1)
            def router():
                def group(j, k):
                    act.wait_ge(turned, j + 1)
                    if not (isinstance(j, int) and j < 2):
                        act.wait_ge(logit_full, j - 1)
                    nc.scalar.copy(stageT[k], arg_bank[k]).then_inc(unturned, 1)
                    for n in range(GRP):
                        nc.scalar.activation(junk[:], xn_all[:, bass.ds(GRP * j + n, 1), 0:D].rearrange("p a d -> p (a d)"), ACT.Square,
                                             accum_out=ssq[:, bass.ds(GRP * j + n, 1)]).then_inc(ssq_done, 1)
                        act.wait_ge(ssq_done, GRP * j + n + 1)
                group(0, 0)
                group(1, 1)
                with act.Fori(1, NG // 2) as i:
                    group(2 * i, 0)
                    group(2 * i + 1, 1)
                nc.scalar.activation(ssq[:], ssq[:], ACT.Ln, bias=epsc[:, 3:4], scale=1.0 / D).then_inc(rr_step, 1)
                act.wait_ge(rr_step, 1)
                nc.scalar.activation(xn_all[:, :, C_RMS], ssq[:], ACT.Exp, scale=-0.5).then_inc(rr_done, 1)
                act.wait_ge(sort_step, 4)
                nc.scalar.activation(grid[1], grid[1], ACT.Exp).then_inc(score_exp, 1)

            def experts():
                def rows_turned(k, q):
                    act.wait_ge(xT_full, k + 1)
                    if not (isinstance(k, int) and k < 2):
                        act.wait_ge(h_full, k - 1)
                    nc.scalar.copy(xfT[:, q % 2, :], sc[:, q % 2, 0, :]).then_inc(xT_done, 1)

                def silu(k, q):
                    act.wait_ge(h_full, k + 1)
                    if not (isinstance(k, int) and k < 2):
                        act.wait_ge(hT_full, k - 1)
                    nc.scalar.activation(hb[:, q % 2, :], arg_bank[q % 2], ACT.Silu).then_inc(h_done, 1)

                nc.scalar.preload_act_table_set("silu_and_others")
                staggered(((2, rows_turned), (1, silu)), act)
                nc.scalar.preload_act_table_set("natural_log_exp_and_others")

            for k in range(2):
                act.wait_ge(mn_full, 3 + k)
                nc.scalar.copy(n_all[:, 512 * k:512 * k + 512], acc[:, k]).then_inc(mn_used, 1)

            def evac(b, r, dst, src):
                act.wait_ge(misc_full, ROUNDS * b + (r + 1))
                nc.scalar.copy(dst, src).then_inc(act_misc, 1)

            def turn(b, k):
                evac(b, R_T, xnT[:, k, :], misc[:, R_T % 2, 0:T])

            def softlog(b, k):
                act.wait_ge(na_done, b + 1)
                nc.scalar.activation(na[:], na[:], ACT.Exp).then_inc(ex_done, 1)
                act.wait_ge(ex_done, b + 1)
                nc.scalar.activation(na[:], na[:], ACT.Ln, bias=epsc[0:CR, 1:2]).then_inc(l1_done, 1)

            def loglam(b, k):
                act.wait_ge(sp_done, b + 1)
                nc.scalar.activation(lnlam[:], zz[:, 0:2, :], ACT.Ln, bias=epsc[0:CR, 2:3]).then_inc(lnlam_done, 1)

            def z_out(b, k, part=range(4)):
                for r in part:
                    evac(b, R_Z + r, zT[:, k, 2 * r:2 * r + 2, :], misc[:, (R_Z + r) % 2, :].rearrange("p (h t) -> p h t", h=2))

            def u_out(b, k):
                for r in range(4):
                    evac(b, R_U + r, u[:, k, r // 2, (r % 2) * 512:(r % 2 + 1) * 512], misc[:, (R_U + r) % 2, :])

            def exps(b, k, n, first):
                ks, qt = UNITS[n]
                m = (3 * k + n) % 2
                act.wait_ge(arg_full, 3 * b + (n + 1))
                if not (first and n < 2):
                    act.wait_ge(mult_done, 6 * b + (2 * n - 2))
                for h in range(H):
                    ins = nc.scalar.activation(expo[:, m, h, :].rearrange("p (a c) -> p a c", a=2), arg[:, :, h, :], ACT.Exp,
                                               bias=negG[:, k, 2 * ks + h // HG, h % HG:h % HG + 1])
                ins.then_inc(exp_done, 1)

            def out_rstd(b):
                act.wait_ge(ostat_done, b + 1)
                nc.scalar.activation(orstd[:], odev[:], ACT.Ln, bias=epsc[:, 0:1], scale=1.0 / D).then_inc(olog_done, 1)
                act.wait_ge(olog_done, b + 1)
                nc.scalar.activation(orstd[:], orstd[:], ACT.Exp, scale=-0.5).then_inc(orstd_done, 1)

            def body(b, k, nxt, first=False):
                c, kn = b + 1, 1 - k
                if nxt:
                    turn(c, kn)
                exps(b, k, 0, first)
                exps(b, k, 1, first)
                if nxt:
                    z_out(c, kn, range(2))
                    softlog(c, kn)
                if not first:
                    out_rstd(b - 1)
                if nxt:
                    z_out(c, kn, range(2, 4))
                exps(b, k, 2, first)
                if nxt:
                    loglam(c, kn)
                if nxt:
                    u_out(c, kn)
                else:
                    out_rstd(b)

            router()
            turn(0, 0)
            softlog(0, 0)
            z_out(0, 0)
            loglam(0, 0)
            u_out(0, 0)
            body(0, 0, True, True)
            body(1, 1, True)
            with act.Fori(1, HALF // 2) as i:
                body(2 * i, 0, True)
                body(2 * i + 1, 1, True)
            experts()
            with act.Fori(HALF // 2, NB // 2 - 1) as i:
                body(2 * i, 0, True)
                body(2 * i + 1, 1, True)
            body(NB - 2, 0, True)
            body(NB - 1, 1, False)

        def moments(dve, st, total, diff, mu, dv, done, c):
            nc.vector.tensor_tensor(diff[:], st[:, :, 1], st[:, :, 4], ALU.subtract).then_inc(done, 1)
            nc.vector.tensor_tensor(total[:], st[:, :, 1:3], st[:, :, 4:6], ALU.add).then_inc(done, 1)
            dve.wait_ge(done, c + 2)
            nc.vector.tensor_tensor(diff[:], diff[:], diff[:], ALU.mult).then_inc(done, 1)
            nc.vector.tensor_scalar(mu[:], total[:, :, 0], 0.5, None, ALU.mult).then_inc(done, 1)
            dve.wait_ge(done, c + 4)
            return nc.vector.scalar_tensor_tensor(out=dv[:], in0=diff[:], scalar=D / 4.0, in1=total[:, :, 1], op0=ALU.mult, op1=ALU.add)

        @block.vector
        def _(dve):
            nc.vector.memset(epsc[:, 0:1], 1e-5).then_inc(const_set, 1)
            nc.vector.memset(epsc[:, 1:2], 1.0).then_inc(const_set, 1)
            nc.vector.memset(ones[:], 1.0).then_inc(const_set, 1)
            nc.vector.memset(ones128[:], 1.0).then_inc(const_set, 1)
            nc.vector.memset(xn_all[:, :, D:XW], 0.0).then_inc(const_set, 1)
            nc.vector.memset(idle0[:], 0.0).then_inc(const_set, 1)
            nc.vector.memset(epsc[:, 3:4], 1e-6).then_inc(const_set, 1)
            nc.vector.memset(epsc[:, 2:3], LAM_MIN).then_inc(const_set, 1)
            for c in range(4):
                dve.wait_ge(xload[c], 16)
                with dve.Fori(c * XC, (c + 1) * XC) as i:
                    nc.vector.bn_stats(stats[:, bass.ds(i, 1), :].rearrange("p a s -> p (a s)"),
                                       x_all[:, bass.ds(i, 1), :].rearrange("p a d -> p (a d)")).then_inc(stat_step, 1)
            dve.wait_ge(stat_step, NT)
            moments(dve, stats, msum, mdif, mean, dev, stats_step, 0).then_inc(stats_done, 1)
            dve.wait_ge(rstd_done, 1)
            with dve.Fori(0, NT) as i:
                nc.vector.tensor_scalar(xn_all[:, bass.ds(i, 1), 0:D].rearrange("p a d -> p (a d)"),
                                        x_all[:, bass.ds(i, 1), :].rearrange("p a d -> p (a d)"),
                                        mean[:, bass.ds(i, 1)],
                                        rstd[:, bass.ds(i, 1)], ALU.subtract, ALU.mult).then_inc(xn_done, 1)
            for k in range(2):
                dve.wait_ge(mn_full, 1 + k)
                nc.vector.tensor_scalar(m_all[:, 4 * k:4 * k + 4, :], sc[:, k], float(D) ** -0.5, None, ALU.mult).then_inc(mn_used, 1)
            dve.wait_ge(loads, LOADS)

            def logits(b, k):
                for r, at in ((R_DL, 0), (R_GATE, 2)):
                    dve.wait_ge(misc_full, ROUNDS * b + (r + 1))
                    for g in range(2):
                        ins = nc.vector.tensor_scalar(zz[:, at + g, :], misc[0:CR, r % 2, g * T:(g + 1) * T], zbias[:, at + g:at + g + 1],
                                                      None, ALU.add)
                        if g == 0:
                            ins.then_inc(zz_done, 1)
                        else:
                            ins.then_inc(dve_misc, 1)
                dve.wait_ge(zz_done, 2 * b + 2)
                dve.wait_ge(dve_misc, len(DVE_ROUNDS) * b + 2)
                nc.vector.scalar_tensor_tensor(out=na[:], in0=zz[:], scalar=-1.0, in1=zz[:], op0=ALU.mult, op1=ALU.min).then_inc(na_done, 1)

            def softplus_scan(b, k):
                dve.wait_ge(l1_done, b + 1)
                nc.vector.scalar_tensor_tensor(out=zz[:], in0=zz[:], scalar=0.0, in1=na[:], op0=ALU.max, op1=ALU.add).then_inc(sp_done, 1)
                dve.wait_ge(sp_done, b + 1)
                for g in range(2):
                    nc.vector.tensor_tensor_scan(gsum[:, g, :], ones[:], zz[:, 2 + g, :], 0.0, ALU.mult, ALU.subtract).then_inc(scan_done, 1)

            def gates_out(b, k):
                dve.wait_ge(misc_full, ROUNDS * b + (R_GT + 1))
                src = misc[:, R_GT % 2, 0:4 * CR].rearrange("p (a c) -> p a c", a=4)[:, :, 0:HG * LV].rearrange("p a (h l) -> p a h l", l=LV)[:, :, :, 0]
                nc.vector.tensor_scalar(negG[:, k], src, -1.0, None, ALU.mult).then_inc(dve_misc, 1)

            def values_out(b, k):
                for r in range(4):
                    dve.wait_ge(misc_full, ROUNDS * b + (R_V + r + 1))
                    nc.vector.tensor_tensor(val[0:VR, k, 2 * r:2 * r + 2, :], misc[0:VR, (R_V + r) % 2, :].rearrange("p (h t) -> p h t", h=2),
                                            own[:].rearrange("p (a t) -> p a t", a=1).broadcast_to([VR, 2, T]), ALU.mult).then_inc(dve_misc, 1)

            def products(b, k, n, first):
                m = (3 * k + n) % 2
                dve.wait_ge(exp_done, 3 * b + (n + 1))
                if not (first and n < 2):
                    dve.wait_ge(av_done, 3 * b + (n - 1))
                for half in range(2):
                    dve.wait_ge(s_full, 6 * b + (2 * n + half + 1))
                    nc.vector.tensor_tensor(att[:, m, 4 * half:4 * half + 4, :], sc[:, half], expo[:, m, 4 * half:4 * half + 4, :],
                                            ALU.mult).then_inc(mult_done, 1)

            def parts(b):
                dve.wait_ge(lnlam_done, b + 1)
                dve.wait_ge(scan_done, 2 * b + 2)
                nc.vector.tensor_tensor(v32[:], lnlam[:], gsum[:], ALU.add).then_inc(part_step, 1)
                for n in range(2):
                    dve.wait_ge(part_step, 4 * b + (2 * n + 1))
                    nc.vector.tensor_copy(vb[:], v32[:]).then_inc(part_step, 1)
                    dve.wait_ge(part_step, 4 * b + (2 * n + 2))
                    ins = nc.vector.scalar_tensor_tensor(out=(v32, vparts)[n][:], in0=vb[:], scalar=minus[:, n:n + 1], in1=v32[:],
                                                         op0=ALU.mult, op1=ALU.add)
                    ins.then_inc(part_step if n == 0 else parts_done, 1)

            def norm_out(b, k):
                dve.wait_ge(av_done, 3 * b + 3)
                if not (isinstance(b, int) and b == 0):
                    dve.wait_ge(y_step, 3 * b)
                nc.vector.tensor_tensor(o[:], acc[:, :, 0:D], xn_all[:, bass.ds(2 * b, 2), 0:D], ALU.add).then_inc(ln_step, 1)
                dve.wait_ge(ln_step, 4 * b + 1)
                for n in range(2):
                    nc.vector.bn_stats(ostats[:, n, :], o[:, n, :]).then_inc(ln_step, 1)
                dve.wait_ge(ln_step, 4 * b + 3)
                moments(dve, ostats, osum, odif, omean, odev, omom_step, 4 * b).then_inc(ostat_done, 1)
                dve.wait_ge(orstd_done, b + 1)
                nc.vector.tensor_scalar(y[:, 0, :], o[:, 0, :], omean[:, 0:1], orstd[:, 0:1], ALU.subtract, ALU.mult).then_inc(ln_step, 1)
                nc.vector.tensor_scalar(y[:, 1, :], o[:, 1, :], omean[:, 1:2], orstd[:, 1:2], ALU.subtract, ALU.mult).then_inc(y_done, 1)

            def body(b, k, nxt, first=False):
                c, kn = b + 1, 1 - k
                products(b, k, 0, first)
                if nxt:
                    logits(c, kn)
                products(b, k, 1, first)
                if not first:
                    norm_out(b - 1, k)
                if nxt:
                    softplus_scan(c, kn)
                products(b, k, 2, first)
                if nxt:
                    parts(c)
                    gates_out(c, kn)
                    values_out(c, kn)
                else:
                    norm_out(b, k)

            def sort():
                count = [0]

                def then(ins):
                    count[0] += 1
                    ins.then_inc(sort_step, 1)
                    dve.wait_ge(sort_step, count[0])

                def te(x):
                    return x.rearrange("p (t e) -> p t e", e=E)

                def over_e(col):
                    return col.rearrange("p (t a) -> p t a", a=1).broadcast_to([P, NT, E])

                def over_t(row, n=NT):
                    return row.rearrange("p (a e) -> p a e", a=1).broadcast_to([P, n, E])

                logit, gap, low, oh, pos, carry = grid[0], grid[1], grid[2], grid[3], grid[4], grid[5]
                top, expert = small64[:, 0, :], small64[:, 1, :]
                total, tiles, ends, starts = small[:, 0], small[:, 1], small[:, 2], small[:, 3]
                dve.wait_ge(logit_full, NG)
                dve.wait_ge(rr_done, 1)
                rms = xn_all[:, :, C_RMS:C_RMS + 1].broadcast_to([P, NT, E])
                then(nc.vector.tensor_tensor(te(logit), te(misc[:, 0, :]), rms, ALU.mult))
                then(nc.vector.tensor_reduce(top, te(logit), AX_X, ALU.max))
                then(nc.vector.tensor_tensor(te(gap), te(logit), over_e(top), ALU.subtract))
                then(nc.vector.tensor_scalar(low, gap, 0.0, float(E), ALU.is_lt, ALU.mult))
                then(nc.vector.tensor_tensor(te(low), te(low), over_t(eid[:]), ALU.add))
                then(nc.vector.tensor_reduce(expert, te(low), AX_X, ALU.min))
                then(nc.vector.tensor_tensor(te(oh), over_t(eid[:]), over_e(expert), ALU.is_equal))
                nc.vector.tensor_copy(onehot, oh).then_inc(onehot_done, 1)
                dve.wait_ge(score_exp, 1)
                then(nc.vector.tensor_reduce(top, te(gap), AX_X, ALU.add))
                then(nc.vector.reciprocal(xn_all[:, :, C_SCORE], top))
                dve.wait_ge(rank_full, 1)
                then(nc.vector.tensor_copy(pos, arg_bank[1]))
                for e in range(E):
                    ins = nc.vector.tensor_tensor_scan(te(carry)[:, :, e], ones128[:, 0:NT], te(pos)[:, :, e], 0.0, ALU.mult, ALU.add)
                    if e < E - 1:
                        ins.then_inc(sort_step, 1)
                        count[0] += 1
                then(ins)
                nc.vector.tensor_copy(total, te(carry)[:, NT - 1, :]).then_inc(sort_step, 1)
                count[0] += 1
                then(nc.vector.tensor_tensor(pos, carry, pos, ALU.subtract))
                kp = kP[:].rearrange("p (a t) -> p a t", a=1).broadcast_to([P, E, NT])
                many = total.rearrange("p (e a) -> p e a", a=1).broadcast_to([P, E, NT])
                g7 = grid[7].rearrange("p (e t) -> p e t", e=E)
                then(nc.vector.tensor_tensor(g7, many, kp, ALU.is_gt))
                then(nc.vector.tensor_reduce(tiles, g7, AX_X, ALU.add))
                then(nc.vector.tensor_tensor_scan(ends, ones128[:, 0:E], tiles, 0.0, ALU.mult, ALU.add))
                then(nc.vector.tensor_tensor(starts, ends, tiles, ALU.subtract))
                then(nc.vector.tensor_scalar(starts, starts, float(P), None, ALU.mult))
                then(nc.vector.tensor_tensor(te(pos), te(pos), over_t(starts), ALU.add))
                then(nc.vector.tensor_tensor(pos, pos, arg_bank[0], ALU.add))
                then(nc.vector.tensor_tensor(pos, pos, oh, ALU.mult))
                then(nc.vector.tensor_reduce(expert, te(pos), AX_X, ALU.add))
                then(nc.vector.tensor_copy(slot[:], expert))
                tg = tgrid.rearrange("p (t e) -> p t e", e=E)
                tid = tileid[:].rearrange("p (t a) -> p t a", a=1).broadcast_to([P, ST, E])
                then(nc.vector.tensor_tensor(tg, over_t(ends, ST), tid, ALU.is_le))
                then(nc.vector.tensor_reduce(texp[:], tg, AX_X, ALU.add))
                then(nc.vector.tensor_scalar(texp[:], texp[:], float(E - 1), None, ALU.min))
                then(nc.vector.tensor_scalar(tsel[:], texp[0:NP3 * E, :], prow[:, 0:1], None, ALU.is_equal))
                nc.vector.tensor_copy(texpi[:], texp[0:1, :]).then_inc(sorted_, 1)

            def experts():
                def scale_rows(k, q):
                    dve.wait_ge(xs_in[q], 16 * ((k - q) // NS) + 16 if isinstance(k, int) else 4 * (k - q) + 16)
                    if not (isinstance(k, int) and k < 2):
                        dve.wait_ge(xT_full, k - 1)
                    nc.vector.tensor_scalar(xf[:, q % 2, :], xs[:, q, 0:D], xs[:, q, C_RMS:C_RMS + 1], None, ALU.mult).then_inc(xf_done, 1)

                def select(k, q):
                    if not (isinstance(k, int) and k < NS):
                        dve.wait_ge(yx_full, k - 3)
                    nc.vector.tensor_scalar(sel[:, q, :], ones128[0:NP3 * E, :], tsel[:, bass.ds(k, 1)], None, ALU.mult).then_inc(sel_done, 1)

                def hidden_turned(k, q):
                    dve.wait_ge(hT_full, k + 1)
                    if not (isinstance(k, int) and k < 2):
                        dve.wait_ge(yx_full, k - 1)
                    nc.vector.tensor_copy(hT[:, q % 2, :], misc[:, q % 2, :]).then_inc(hT_done, 1)

                def output(k, q):
                    dve.wait_ge(yx_full, k + 1)
                    if not (isinstance(k, int) and k < NS):
                        dve.wait_ge(y_out[q], 16 * ((k - q) // NS) if isinstance(k, int) else 4 * (k - q))
                    nc.vector.tensor_copy(yb[:, q, :], acc[:, q % 2, D:2 * D]).then_inc(yx_done, 1)

                staggered(((3, scale_rows), (2, select), (0, hidden_turned), (-1, output)), dve)

            nc.vector.memset(rowst[:, 0, :], 0.0).then_inc(zero_set, 1)
            sort()
            logits(0, 0)
            softplus_scan(0, 0)
            parts(0)
            gates_out(0, 0)
            values_out(0, 0)
            body(0, 0, True, True)
            body(1, 1, True)
            with dve.Fori(1, HALF // 2) as i:
                body(2 * i, 0, True)
                body(2 * i + 1, 1, True)
            experts()
            with dve.Fori(HALF // 2, NB // 2 - 1) as i:
                body(2 * i, 0, True)
                body(2 * i + 1, 1, True)
            body(NB - 2, 0, True)
            body(NB - 1, 1, False)

        @block.gpsimd
        def _(pool):
            def pair(t):
                return t[:].rearrange("p (a d) -> p a d", a=1).broadcast_to([P, 2, D])

            def stage_x(b):
                nc.gpsimd.tensor_copy(xnb[:], xn_all[:, bass.ds(2 * b, 2), 0:D]).then_inc(xnb_done, 1)

            def finish(b):
                pool.wait_ge(y_done, b + 1)
                pool.wait_ge(ln_step, 4 * b + 4)
                nc.gpsimd.tensor_tensor(y[:], y[:], pair(lng), ALU.mult).then_inc(y_step, 1)
                pool.wait_ge(y_step, 3 * b + 1)
                nc.gpsimd.tensor_tensor(y[:], y[:], pair(lnb), ALU.add).then_inc(y_step, 1)
                pool.wait_ge(y_step, 3 * b + 2)
                xb = x_all[:, bass.ds(2 * b, 2), :]
                nc.gpsimd.tensor_tensor(xb, xb, y[:], ALU.add).then_inc(y_step, 1)

            def carry_wait():
                nc.gpsimd.tensor_tensor(idle[:], idle0[:], idle0[:], ALU.add)

            def send_rows(b):
                for q in range(4):
                    if not isinstance(b, int):
                        pool.wait_ge(row_out[q], 16 * b)
                    nc.gpsimd.tensor_copy(rowst[:, q:q + 1, :], xn_all[:, bass.ds(4 * b + q, 1), :]).then_inc(row_copy, 1)
                    nc.gpsimd.tensor_copy(slotst[:, q:q + 1], slot[:, bass.ds(4 * b + q, 1)]).then_inc(row_copy, 1)
                    pool.wait_ge(row_copy, 8 * b + (2 * q + 2))
                    carry_wait()
                    nc.gpsimd.indirect_dma_start(out=rows_dram, out_offset=bass.IndirectOffsetOnAxis(ap=slotst[:, q:q + 1], axis=0),
                                                 in_=rowst[:, q, :], in_offset=None).then_inc(row_out[q], 16)

            def fetch_rows(b):
                for q in range(4):
                    nc.gpsimd.tensor_copy(slotst[:, q:q + 1], slot[:, bass.ds(4 * (b - HALF) + q, 1)]).then_inc(slot_copy, 1)
                    pool.wait_ge(slot_copy, 4 * b + (q + 1 - 4 * HALF))
                    carry_wait()
                    nc.gpsimd.indirect_dma_start(out=got[:, q, :], out_offset=None, in_=y_dram,
                                                 in_offset=bass.IndirectOffsetOnAxis(ap=slotst[:, q:q + 1], axis=0)).then_inc(got_in[q], 16)

            def add_rows(b):
                pool.wait_ge(y_step, 3 * b)
                for q in range(4):
                    pool.wait_ge(got_in[q], 16 * b + (16 - 16 * HALF))
                    xb = x_all[:, bass.ds(4 * (b - HALF) + q, 1), :]
                    score = xn_all[:, bass.ds(4 * (b - HALF) + q, 1), C_SCORE:C_SCORE + 1].broadcast_to([P, 1, D])
                    nc.gpsimd.tensor_tensor(got[:, q:q + 1, :], got[:, q:q + 1, :], score, ALU.mult).then_inc(got_scored, 1)
                    pool.wait_ge(got_scored, 4 * b + (q + 1 - 4 * HALF))
                    nc.gpsimd.tensor_tensor(xb, xb, got[:, q:q + 1, :], ALU.add).then_inc(got_added, 1)

            def body(b, half, first=False, more=True):
                if not first:
                    finish(b - 1)
                if half:
                    fetch_rows(b)
                else:
                    send_rows(b)
                if more:
                    pool.wait_ge(misc_full, ROUNDS * b + (ROUNDS + 1))
                    stage_x(b + 2)
                if half:
                    add_rows(b)

            pool.wait_ge(loads, LOADS)
            bw = lambda c: prow[:, c:c + 1].broadcast_to([NP3 * E, F + D])
            steps = [(bparts, bias32, None), (biasr, bparts, 1), (bias32, bias32, biasr), (bparts, bias32, None),
                     (biasr, bparts, 2), (bparts, bias32, biasr)]
            for n, (dst, src, by) in enumerate(steps):
                if by is None:
                    ins = nc.gpsimd.tensor_copy(dst[:], src[:])
                elif isinstance(by, int):
                    ins = nc.gpsimd.tensor_tensor(dst[:], src[:], bw(by), ALU.mult)
                else:
                    ins = nc.gpsimd.tensor_tensor(dst[:], src[:], by[:], ALU.add)
                ins.then_inc(bias_step, 1)
                pool.wait_ge(bias_step, n + 1)
            nc.gpsimd.tensor_scalar(gate[:], gate[:], rmsw[:, 0:1], None, ALU.mult).then_inc(gate_ready, 1)

            def stage_group(j, k):
                pool.wait_ge(xn_done, GRP * j + GRP)
                if not (isinstance(j, int) and j < 2):
                    pool.wait_ge(turned, j - 1)
                nc.gpsimd.tensor_copy(stage[k], xn_all[:, bass.ds(GRP * j, GRP), 0:D]).then_inc(staged, 1)
            stage_group(0, 0)
            stage_group(1, 1)
            with pool.Fori(1, NG // 2) as i:
                stage_group(2 * i, 0)
                stage_group(2 * i + 1, 1)
            pool.wait_ge(w1_loaded, 32)
            nc.gpsimd.tensor_scalar(wstage[:].rearrange("p a b -> p (a b)"), wstage[:].rearrange("p a b -> p (a b)"), rmsw[:, 0:1], None,
                                    ALU.mult).then_inc(w1_ready, 1)
            pool.wait_ge(const_set, 8)
            pool.wait_ge(xn_done, NT)
            stage_x(0)
            pool.wait_ge(misc_full, 1)
            stage_x(1)
            pool.wait_ge(sorted_, 1)
            pool.wait_ge(zeroed, 16)
            body(0, False, first=True)
            with pool.Fori(1, HALF) as i:
                body(i, False)
            for q in range(NS):
                pool.wait_ge(y_out[q], 16 * (ST // NS))
            body(HALF, True)
            with pool.Fori(HALF + 1, NB - 2) as i:
                body(i, True)
            body(NB - 2, True, more=False)
            body(NB - 1, True, more=False)
            pool.wait_ge(got_added, 4 * HALF)
            finish(NB - 1)


NAMES = ["x", "wdl", "wg", "zbias", "lng", "lnb", "w4", "c_level", "c_own", "c_causal", "c_rep", "c_minus", "c_ident",
         "gate", "rmsw", "bias", "w1", "w2", "c_before", "c_all", "c_eid", "c_kP", "c_tile", "c_prow"]


def kernel(**inputs):
    import numpy as _np
    import concourse.bacc as _bacc
    from concourse import mybir as _mybir
    from concourse.bass_utils import run_bass_kernel_spmd as _run

    g = {n: _np.asarray(v) for n, v in inputs.items()}
    wdl = g["L0_attn_Wdl"].reshape(H, 12, D)[:, :LV].reshape(2, HG * LV, D)
    wgr = _np.repeat(g["L0_attn_Wg"], LV, axis=0).reshape(2, HG * LV, D)
    lp = g["L0_attn_Lparam"][:, :LV].reshape(2, HG * LV)
    bg = _np.repeat(g["L0_attn_bg"], LV).reshape(2, HG * LV)
    rows = lambda w: _np.tile(w, (1, NP3, 1)).transpose(2, 0, 1).reshape(D, 2 * CR)
    by_head = lambda w: w.reshape(H, D, D).transpose(1, 0, 2).reshape(D, H * D)
    data = {
        "x": g["L0_attn_x"].reshape(NB * T, D),
        "wdl": rows(wdl), "wg": rows(wgr),
        "zbias": _np.tile(_np.concatenate([lp, bg]), (1, NP3)).T,
        "lng": _np.tile(g["L0_attn_ln_g"][None], (P, 1)), "lnb": _np.tile(g["L0_attn_ln_b"][None], (P, 1)),
        "w4": _np.stack([by_head(g["L0_attn_Wq"]), by_head(g["L0_attn_Wk"]), by_head(g["L0_attn_Wv"]),
                         by_head(g["L0_attn_Wo"].T)]),
        "gate": g["L0_ffn_gate_w"].T, "rmsw": g["L0_ffn_rms_w"][:, None],
        "bias": _np.tile(_np.concatenate([g["L0_ffn_b1"], g["L0_ffn_b2"]], 1), (NP3, 1)),
        "w1": g["L0_ffn_W1"].transpose(1, 0, 2).reshape(D, E * F),
        "w2": g["L0_ffn_W2"].reshape(E, FT, P, D).transpose(2, 0, 1, 3).reshape(P, E * FT * D),
        **level_constants(),
    }
    nc = _bacc.Bacc("TRN2", target_bir_lowering=False, num_devices=1)
    arrays, args = {}, {}
    for name in NAMES:
        v = _np.ascontiguousarray(data[name])
        arrays[f"in_{name}"] = v
        args[name] = nc.dram_tensor(f"in_{name}", v.shape, _mybir.dt.from_np(v.dtype), kind="ExternalInput").ap()
    out = nc.dram_tensor("out_0", (NB * T, D), _mybir.dt.from_np(_np.dtype("float32")), kind="ExternalOutput").ap()
    build(nc, args, out)
    r = _run(nc, [arrays], core_ids=[0])
    return r.results[0]["out_0"].reshape(NB, T, D)
```

```python
from contextlib import ExitStack

import concourse.bass as bass
import numpy as np
from concourse import mybir

ALU = mybir.AluOpType
ACT = mybir.ActivationFunctionType
F32 = mybir.dt.float32
F32R = mybir.dt.float32r
I32 = mybir.dt.int32
U32 = mybir.dt.uint32
BF16 = mybir.dt.bfloat16
U16 = mybir.dt.uint16
AX_X = mybir.AxisListType.X

P = 128
NB, T, D = 32, 256, 128
H = 8
LV = 9
TW = 4
NP3 = 3
HG = 4
VR = NP3 * TW * LV
CR = NP3 * HG * LV
KR = VR + TW
LW = T - TW + P
NT = NB * T // P
E, F = 8, 512
FT = F // P
BIG = -1.0e30
LAM_MIN = 2.0 ** -63
UNITS = [(0, 0), (0, 1), (1, 1)]
VC = H * LV
PREPARE = ["T0", "DL0", "Z0", "Z1", "Z2", "Z3", "T1", "GT", "V0", "V1", "V2", "V3", "DL1"]
BESIDE = ["U0", "U1", "GT", "U2", "U3", "T", "Z0", "Z1", "Z2", "V0", "V1", "V2", "Z3", "V3", "DL"]
BANKS = 3
HALF = NB // 2
XW = D + 4
C_RMS, C_SCORE = D, D + 1
ST = NT + E
GRP = 4
NG = NT // GRP
CONSTS = 8
NS = 4


def bf16_bits(a):
    return (np.ascontiguousarray(a, np.float32).view(np.uint32) >> 16).astype(np.uint16)


def level_constants():
    d = np.arange(TW)[:, None] - (np.arange(LW)[None, :] - (T - TW))
    lvl = np.where(d <= 0, 0, np.floor(np.log2(np.maximum(d, 1))).astype(int) + 1)
    m = np.zeros((KR, LW), np.float32)
    for p in range(NP3):
        for q in range(TW):
            for l in range(LV):
                m[(p * TW + q) * LV + l] = (d[q] >= 0) & (lvl[q] == l)
    m[VR:] = d < 0
    own = np.zeros((VR, T), np.float32)
    for r in range(VR):
        own[r] = np.arange(T) % TW == (r // LV) % TW
    causal = np.zeros((TW, H, T), np.float32)
    for q in range(TW):
        causal[q, :, q::TW] = BIG
    rep = np.zeros((CR, HG, VR), np.float32)
    for p in range(NP3):
        for h in range(HG):
            for q in range(TW):
                for l in range(LV):
                    rep[(p * HG + h) * LV + l, h, (p * TW + q) * LV + l] = 1
    return {
        "c_level": bf16_bits(m), "c_own": own, "c_causal": bf16_bits(causal.reshape(TW, H * T)),
        "c_before": bf16_bits(np.triu(np.ones((P, P), np.float32), 1)), "c_all": bf16_bits(np.ones((P, P), np.float32)),
        "c_eid": np.tile(np.arange(E, dtype=np.float32), (P, 1)), "c_kP": np.tile(P * np.arange(NT, dtype=np.float32), (P, 1)),
        "c_tile": np.tile(np.arange(ST, dtype=np.float32), (P, 1)),
        "c_prow": np.stack([np.arange(NP3 * E) % E, -1.0 * (np.arange(NP3 * E) >= E), -1.0 * (np.arange(NP3 * E) >= 2 * E)], 1).astype(np.float32),
        "c_rep": bf16_bits(rep.reshape(CR, HG * VR)), "c_ident": np.eye(P, dtype=np.float32),
    }


def build(nc, a, out):
    ctx = ExitStack()
    with ctx:
        def sb(name, shape, dt=F32):
            return ctx.enter_context(nc.sbuf_tensor(name, shape, dt))

        def psum(name, shape):
            return ctx.enter_context(nc.psum_tensor(name, shape, F32))

        def sem(name):
            return ctx.enter_context(nc.semaphore(name))

        level = sb("level", [KR, LW], BF16)
        own = sb("own", [VR, T])
        rep = sb("rep", [CR, HG, VR], BF16)
        ident = sb("ident", [P, P])
        before = sb("before", [P, P], BF16)
        allones = sb("allones", [P, P], BF16)
        eid = sb("eid", [P, E])
        kP = sb("kP", [P, NT])
        tileid = sb("tileid", [P, ST])
        prow = sb("prow", [NP3 * E, 3])
        ones128 = sb("ones128", [P, P])
        ones = sb("ones", [VC, T])
        consts = sb("consts", [P, 4])
        idle0 = sb("idle0", [1, 1])
        idle = sb("idle", [1, 1])
        wlog = sb("wlog", [P, 2 * VC])
        wlog_p = sb("wlog_p", [P, 2, 2 * VC], F32R)
        zbias = sb("zbias", [VC, 2])
        lng = sb("lng", [P, D])
        lnb = sb("lnb", [P, D])
        wstage = sb("wstage", [P, 4, H * D])
        w1 = wstage[:].rearrange("p a b -> p (a b)").rearrange("p (e f) -> p e f", e=E)
        w2 = sb("w2", [P, E, FT, D])
        m_p = sb("m_p", [P, 2, H, D], F32R)
        n_p = sb("n_p", [P, 2, H * D], F32R)
        gate = sb("gate", [P, E])
        rmsw = sb("rmsw", [P, 1])
        bparts = sb("bparts", [NP3 * E, F + D], BF16)
        xn_all = sb("xn_all", [P, NT, XW])
        ssum = sb("ssum", [P, NT])
        mean = sb("mean", [P, NT])
        dev = sb("dev", [P, NT])
        lnv = sb("lnv", [P, NT])
        rstd = sb("rstd", [P, NT])
        msq = sb("msq", [P, NT])
        slot = sb("slot", [P, NT], U32)
        texp = sb("texp", [P, ST])
        texpi = sb("texpi", [1, ST], I32)
        tsel = sb("tsel", [NP3 * E, ST])
        small = sb("small", [P, 8, E])
        small64 = sb("small64", [P, 2, NT])
        rowst = sb("rowst", [P, 4, XW])
        slotst = sb("slotst", [P, 4], U32)
        got = sb("got", [P, 4, D])
        base = sb("base", [P, 2, 4, D])
        xnb = sb("xnb", [P, 2, D])
        xT_p = sb("xT_p", [P, 2, 2, T], F32R)
        z_p = sb("z_p", [P, 2, H, T], F32R)
        u_p = sb("u_p", [P, 2, 2, H * D], F32R)
        val = sb("val", [KR, H, T], BF16)
        negG = sb("negG", [P, 2, 2, H])
        zz = sb("zz", [VC, 2, T])
        na = sb("na", [VC, 2, T])
        gsum = sb("gsum", [VC, T])
        lnlam = sb("lnlam", [VC, T])
        v32 = sb("v32", [VC, T])
        p3 = sb("p3", [VC, NP3, T], BF16)
        vparts = sb("vparts", [CR, 2, T], BF16)
        expo = sb("expo", [P, 2, H, P])
        att = sb("att", [P, 2, H, P])
        att_h = sb("att_h", [P, 2, H, P], F32R)
        att_l = sb("att_l", [P, 2, H, P], F32R)
        o = sb("o", [P, 2, D])
        ostats = sb("ostats", [P, 2, 6])
        osum = sb("osum", [P, 2, 2])
        odif = sb("odif", [P, 2])
        omean = sb("omean", [P, 2])
        odev = sb("odev", [P, 2])
        orstd = sb("orstd", [P, 2])
        y = sb("y", [P, 2, D])

        eflat = expo[:].rearrange("p k h t -> p (k h t)")
        aflat = att[:].rearrange("p k h t -> p (k h t)")
        squares = eflat
        stageT = [aflat[:, 512 * k:512 * k + 512] for k in range(2)]
        grid = [(eflat, aflat)[k // 4][:, 512 * (k % 4):512 * (k % 4) + 512] for k in range(8)]
        onehot = grid[6][:, 0:NT * E // 2].bitcast(BF16)
        tgrid = eflat[:, 0:ST * E]
        bias32 = sb("bias32", [NP3 * E, F + D])
        biasr = sb("biasr", [NP3 * E, F + D])[:]
        xs = eflat[:, 0:NS * XW].rearrange("p (k d) -> p k d", k=NS)
        xf = eflat[:, 528:528 + 2 * D].rearrange("p (k d) -> p k d", k=2)
        hb = eflat[:, 1024:1024 + 2 * F].rearrange("p (k f) -> p k f", k=2)
        hT = aflat[:, 0:2 * F].rearrange("p (k f) -> p k f", k=2)
        xfT = aflat[:, 1024:1024 + 2 * D].rearrange("p (k d) -> p k d", k=2)
        sel = aflat[0:NP3 * E, 1280:1280 + NS * D // 2].bitcast(BF16).rearrange("p (k d) -> p k d", k=NS)
        yb = got

        misc = psum("misc", [P, BANKS, 512])
        arg = psum("arg", [P, 2, H, 64])
        sc = psum("sc", [P, 2, 4, P])
        acc = psum("acc", [P, 4, D])
        arg_bank = [arg[:, k].rearrange("p h t -> p (h t)") for k in range(2)]
        ybank = [acc[:, 2, :], misc[:, 2, 0:D]]

        def staggered(stages, eng):
            low, high = -3, ST + 1
            start, end = NS, (ST - NS) // NS * NS

            def step(k, q, static):
                for off, stage_ in stages:
                    if not static or 0 <= k + off < ST:
                        stage_(k + off, (q + off) % NS)

            for k in range(low, start):
                step(k, k % NS, True)
            with eng.Fori(start // NS, end // NS) as i:
                for q in range(NS):
                    step(NS * i + q, q, False)
            for k in range(end, high):
                step(k, k % NS, True)

        def rounds_of(b):
            if b is None:
                return PREPARE
            if isinstance(b, int) and b == NB - 1:
                return [r for r in BESIDE if r[0] == "U"]
            if isinstance(b, int) and b == NB - 2:
                return [r for r in BESIDE if r not in ("T", "DL")]
            return BESIDE

        def cut(rounds):
            return [r for r in rounds if r[0] in "TUZ"]

        def count_before(b, full, prepare, short):
            if b is None:
                return 0
            return full * b + (prepare - (short if isinstance(b, int) and b == NB - 1 else 0))

        def nth(b, r):
            return count_before(b, len(BESIDE), len(PREPARE), 2) + rounds_of(b).index(r)

        def nth_cut(b, r):
            return count_before(b, len(cut(BESIDE)), len(cut(PREPARE)), 1) + cut(rounds_of(b)).index(r)

        def bank(b, r):
            shift = 2 if isinstance(b, int) and b == NB - 1 else 0
            return rounds_of(b).index(r) % BANKS if b is None else (len(PREPARE) - shift + rounds_of(b).index(r)) % BANKS

        assert len(BESIDE) % BANKS == 0

        w_in = sem("w_in")
        wstage_in = sem("wstage_in")
        base_in0 = sem("base_in0")
        base_in1 = sem("base_in1")
        base_out0 = sem("base_out0")
        base_out1 = sem("base_out1")
        const_set = sem("const_set")
        bias_step = sem("bias_step")
        gate_ready = sem("gate_ready")
        chunk_step = sem("chunk_step")
        sq_done = sem("sq_done")
        ssq_done = sem("ssq_done")
        rstd_step = sem("rstd_step")
        rstd_done = sem("rstd_done")
        xn_done = sem("xn_done")
        rr_step = sem("rr_step")
        rr_done = sem("rr_done")
        turned = sem("turned")
        unturned = sem("unturned")
        logit_full = sem("logit_full")
        sort_step = sem("sort_step")
        score_exp = sem("score_exp")
        onehot_done = sem("onehot_done")
        rank_full = sem("rank_full")
        sorted_ = sem("sorted_")
        zero_set = sem("zero_set")
        zeroed = sem("zeroed")
        mn_full = sem("mn_full")
        n_high = sem("n_high")
        mn_step = sem("mn_step")
        mn_used = sem("mn_used")
        wlog_step = sem("wlog_step")
        w1_in = sem("w1_in")
        w1_ready = sem("w1_ready")
        xnb_done = sem("xnb_done")
        misc_full = sem("misc_full")
        high_done = sem("high_done")
        misc_used = sem("misc_used")
        zz_done = sem("zz_done")
        ex_done = sem("ex_done")
        l1_done = sem("l1_done")
        sp_done = sem("sp_done")
        lnlam_done = sem("lnlam_done")
        scan_done = sem("scan_done")
        part_step = sem("part_step")
        parts_done = sem("parts_done")
        vrows = sem("vrows")
        arg_full = sem("arg_full")
        exp_done = sem("exp_done")
        s_full = sem("s_full")
        mult_done = sem("mult_done")
        att_high = sem("att_high")
        low_pool = sem("low_pool")
        low_dve = sem("low_dve")
        av_done = sem("av_done")
        ln_step = sem("ln_step")
        omom_step = sem("omom_step")
        ostat_done = sem("ostat_done")
        olog_done = sem("olog_done")
        orstd_done = sem("orstd_done")
        y_done = sem("y_done")
        y_step = sem("y_step")
        scored = sem("scored")
        res_done = sem("res_done")
        row_copy = sem("row_copy")
        slot_copy = sem("slot_copy")
        xf_done = sem("xf_done")
        sel_done = sem("sel_done")
        xT_full = sem("xT_full")
        xT_done = sem("xT_done")
        h_full = sem("h_full")
        h_done = sem("h_done")
        hT_full = sem("hT_full")
        hT_done = sem("hT_done")
        yx_full = sem("yx_full")
        yx_done = sem("yx_done")
        x_in = [sem(f"x_in{c}") for c in range(4)]
        row_out = [sem(f"row_out{q}") for q in range(4)]
        xs_in = [sem(f"xs_in{q}") for q in range(NS)]
        y_out = [sem(f"y_out{q}") for q in range(NS)]
        got_in = [sem(f"got_in{q}") for q in range(4)]
        base_in, base_out = [base_in0, base_in1], [base_out0, base_out1]

        x_dram = a["x"].rearrange("(n p) d -> p n d", p=P)
        out_dram = out.rearrange("(n p) d -> p n d", p=P)
        rows_dram = nc.dram_tensor("rows_by_slot", (ST * P, XW), F32, kind="Internal").ap()
        y_dram = nc.dram_tensor("y_by_slot", (ST * P, D), F32, kind="Internal").ap()
        rows_tiles = rows_dram.rearrange("(n p) d -> p n d", p=P)
        y_tiles = y_dram.rearrange("(n p) d -> p n d", p=P)
        XC = NT // 4

        block = ctx.enter_context(nc.Block())

        W_IN = 19 * 16

        @block.sync
        def _(sp):
            def chunk(c):
                sp.dma_start(xn_all[:, c * XC:(c + 1) * XC, 0:D], x_dram[:, c * XC:(c + 1) * XC, :]).then_inc(x_in[c], 16)

            def flat(t):
                names = " ".join("abcd"[:len(t.shape) - 1])
                return t[:] if len(t.shape) == 2 else t[:].rearrange(f"p {names} -> p ({names})")

            chunk(0)
            chunk(1)
            for dst, name in ((ident, "c_ident"), (gate, "gate"), (rmsw, "rmsw"), (prow, "c_prow"), (bias32, "bias"), (eid, "c_eid"),
                              (kP, "c_kP"), (tileid, "c_tile"), (own, "c_own"), (zbias, "zbias"), (lng, "lng"), (lnb, "lnb"),
                              (wlog, "wlog")):
                sp.dma_start(dst[:], a[name]).then_inc(w_in, 16)
            for dst, name in ((before, "c_before"), (allones, "c_all"), (level, "c_level"), (rep, "c_rep")):
                sp.dma_start(flat(dst), a[name].bitcast(BF16)).then_inc(w_in, 16)
            sp.dma_start(val[VR:KR].rearrange("p h t -> p (h t)"), a["c_causal"].bitcast(BF16)).then_inc(w_in, 16)
            sp.dma_start(flat(w2), a["w2"]).then_inc(w_in, 16)
            chunk(2)
            chunk(3)
            for k in range(4):
                sp.dma_start(wstage[:, k, :], a["w4"][k]).then_inc(wstage_in, 16)

            def load_base(b, k, half):
                for n in range(2):
                    if half and n == 1:
                        sp.dma_start(base[:, k, 2:4, :], out_dram[:, bass.ds(2 * b - NB, 2), :]).then_inc(base_in[k], 16)
                    elif half:
                        sp.dma_start(base[:, k, 0:2, :], x_dram[:, bass.ds(2 * b, 2), :]).then_inc(base_in[k], 16)
                    else:
                        sp.dma_start(base[:, k, n:n + 1, :], x_dram[:, bass.ds(2 * b + n, 1), :]).then_inc(base_in[k], 16)

            def store(b, i, k, half):
                if half:
                    sp.wait_ge(res_done, 2 * b - (NB - 2))
                    sp.dma_start(out_dram[:, bass.ds(2 * b, 2), :], base[:, k, 0:2, :]).then_inc(base_out[k], 16)
                    sp.dma_start(out_dram[:, bass.ds(2 * b - NB, 2), :], base[:, k, 2:4, :]).then_inc(base_out[k], 16)
                else:
                    sp.wait_ge(y_step, 3 * b + 3)
                    for n in range(2):
                        sp.dma_start(out_dram[:, bass.ds(2 * b + n, 1), :], base[:, k, n:n + 1, :]).then_inc(base_out[k], 16)
                sp.wait_ge(base_out[k], 32 * i + 32)

            def value_rows(c):
                sp.wait_ge(parts_done, c + 1)
                for p in range(NP3):
                    for g in range(2):
                        n = HG * LV
                        sp.dma_start(vparts[p * n:(p + 1) * n, g, :], p3[g * n:(g + 1) * n, p, :]).then_inc(vrows, 16)

            load_base(0, 0, False)
            load_base(1, 1, False)
            sp.wait_ge(mn_full, 4)
            sp.dma_start(flat(wstage), a["w1"]).then_inc(w1_in, 16)
            sp.wait_ge(zero_set, 1)
            sp.dma_start(rows_tiles, rowst[:, 0:1, :].broadcast_to([P, ST, XW])).then_inc(zeroed, 16)
            value_rows(0)

            def body(b, i, k, stored_half, loaded_half):
                value_rows(b + 1)
                store(b - 1, i - (1 - k), 1 - k, stored_half)
                load_base(b + 1, 1 - k, loaded_half)

            value_rows(1)
            body(1, 0, 1, False, False)
            with sp.Fori(1, HALF // 2 - 1) as i:
                body(2 * i, i, 0, False, False)
                body(2 * i + 1, i, 1, False, False)
            body(HALF - 2, HALF // 2 - 1, 0, False, False)
            body(HALF - 1, HALF // 2 - 1, 1, False, True)

            for q in range(4):
                sp.wait_ge(row_out[q], 16 * HALF)
            sp.wait_ge(av_done, 3 * HALF)
            for q in range(NS):
                sp.dma_start(xs[:, q, :], rows_tiles[:, q, :]).then_inc(xs_in[q], 16)
            for q in range(NS):
                sp.wait_ge(xf_done, q + 1)
                sp.dma_start(xs[:, q, :], rows_tiles[:, NS + q, :]).then_inc(xs_in[q], 16)

            def exchange(k, q, last):
                sp.wait_ge(yx_done, k + 1)
                sp.dma_start(y_tiles[:, bass.ds(k, 1), :], yb[:, q:q + 1, :]).then_inc(y_out[q], 16)
                if not last:
                    sp.wait_ge(xf_done, k + (NS + 1))
                    sp.dma_start(xs[:, q:q + 1, :], rows_tiles[:, bass.ds(k + 2 * NS, 1), :]).then_inc(xs_in[q], 16)

            with sp.Fori(0, ST // NS - 2) as i:
                for q in range(NS):
                    exchange(NS * i + q, q, False)
            for k in range(ST - 2 * NS, ST):
                exchange(k, k % NS, True)

            body(HALF, HALF // 2, 0, False, True)
            body(HALF + 1, HALF // 2, 1, True, True)
            with sp.Fori(HALF // 2 + 1, NB // 2 - 1) as i:
                body(2 * i, i, 0, True, True)
                body(2 * i + 1, i, 1, True, True)
            body(NB - 2, NB // 2 - 1, 0, True, True)
            store(NB - 2, NB // 2 - 1, 0, True)
            store(NB - 1, NB // 2 - 1, 1, True)

        @block.tensor
        def _(pe):
            def three_passes(dst, lhs, rhs):
                nc.tensor.matmul(dst, lhs(0), rhs(0), start=True, stop=False)
                nc.tensor.matmul(dst, lhs(0), rhs(1), start=False, stop=False)
                return nc.tensor.matmul(dst, lhs(1), rhs(0), start=False, stop=True)

            def mn_products():
                pe.wait_ge(wstage_in, 64)
                for k in range(4):
                    src = 2 * (k // 2)
                    for q in range(4):
                        h = 4 * (k % 2) + q
                        dst = (sc[:, k % 2] if k < 2 else misc[:, k - 1, :].rearrange("p (h d) -> p h d", d=D))[:, q]
                        mm = nc.tensor.matmul(dst, wstage[:, src, h * D:(h + 1) * D], wstage[:, src + 1, h * D:(h + 1) * D],
                                              start=True, stop=True)
                    mm.then_inc(mn_full, 1)

            def router(groups):
                for j in groups:
                    pe.wait_ge(xn_done, j * GRP // XC + 1)
                    for n in range(GRP):
                        mm = nc.tensor.transpose(arg_bank[j % 2][:, n * P:(n + 1) * P], xn_all[:, j * GRP + n, 0:D], ident[:])
                    mm.then_inc(turned, 1)
                    if j >= 1:
                        logit_group(j - 1)
                if groups[-1] == NG - 1:
                    logit_group(NG - 1)

            def logit_group(j):
                pe.wait_ge(unturned, j + 1)
                for n in range(GRP):
                    at = (j * GRP + n) * E
                    mm = nc.tensor.matmul(acc[:].rearrange("p a d -> p (a d)")[:, at:at + E], stageT[j % 2][:, n * P:(n + 1) * P], gate[:],
                                          start=True, stop=True, skip_group_check=True)
                mm.then_inc(logit_full, 1)

            def ranks():
                pe.wait_ge(onehot_done, 1)
                nc.tensor.matmul(arg_bank[0], before[:], onehot, start=True, stop=True)
                nc.tensor.matmul(arg_bank[1], allones[:], onehot, start=True, stop=True).then_inc(rank_full, 1)

            def free_bank(b, r):
                if not (b is None and nth(b, r) < BANKS):
                    pe.wait_ge(misc_used, nth(b, r) - (BANKS - 1))

            def r_turn(b, r, c):
                pe.wait_ge(xnb_done, c + 1)
                free_bank(b, r)
                for n in range(2):
                    mm = nc.tensor.transpose(misc[:, bank(b, r), n * P:(n + 1) * P], xnb[:, n], ident[:])
                mm.then_inc(misc_full, 1)

            def r_logits(b, r, k, turn):
                pe.wait_ge(misc_used, nth(b, turn) + 1)
                free_bank(b, r)
                for g in range(2):
                    mm = three_passes(misc[0:VC, bank(b, r), g * T:(g + 1) * T], lambda p: wlog_p[:, p, g * VC:(g + 1) * VC],
                                      lambda p: xT_p[:, k, p, :])
                mm.then_inc(misc_full, 1)

            def r_z(b, k, part):
                for n in part:
                    r = f"Z{n}"
                    free_bank(b, r)
                    for q in range(2):
                        mm = three_passes(misc[:, bank(b, r), q * T:(q + 1) * T], lambda p: m_p[:, p, 2 * n + q, :],
                                          lambda p: xT_p[:, k, p, :])
                    mm.then_inc(misc_full, 1)

            def r_u(b, k, part):
                for n in part:
                    r = f"U{n}"
                    free_bank(b, r)
                    ks, half = n // 2, n % 2
                    three_passes(misc[:, bank(b, r), :], lambda p: xT_p[:, k, p, ks * P:(ks + 1) * P],
                                 lambda p: n_p[:, p, half * 512:(half + 1) * 512]).then_inc(misc_full, 1)

            def r_gt(b, c):
                pe.wait_ge(scan_done, c + 1)
                free_bank(b, "GT")
                for n in range(2):
                    mm = nc.tensor.transpose(misc[:, bank(b, "GT"), n * VC:(n + 1) * VC], gsum[:, n * P:(n + 1) * P], ident[0:VC, 0:VC])
                mm.then_inc(misc_full, 1)

            def r_v(b, c, part=range(4)):
                pe.wait_ge(vrows, NP3 * 2 * 16 * c + NP3 * 2 * 16)
                for n in part:
                    r = f"V{n}"
                    free_bank(b, r)
                    for q in range(2):
                        h = 2 * n + q
                        mm = nc.tensor.matmul(misc[0:VR, bank(b, r), q * T:(q + 1) * T], rep[:, h % HG, :], vparts[:, h // HG, :],
                                              start=True, stop=True)
                    mm.then_inc(misc_full, 1)

            def arguments(b, k, n, first):
                ks, qt = UNITS[n]
                if n == 0:
                    pe.wait_ge(misc_used, nth(None if first else b - 1, "V3") + 1)
                if not (first and n == 0):
                    pe.wait_ge(exp_done, 3 * b + n)
                for j in range(P // TW):
                    t = qt * P + j * TW
                    w = T - TW - (t - ks * P)
                    mm = nc.tensor.matmul(arg[:, j // 16, :, (j % 16) * TW:(j % 16 + 1) * TW], level[:, w:w + P],
                                          val[:, :, t:t + TW], start=(j % 16 == 0), stop=True, skip_group_check=True)
                mm.then_inc(arg_full, 1)

            def scores(b, k, n, first):
                ks, qt = UNITS[n]
                for half in range(2):
                    if not (first and n == 0):
                        pe.wait_ge(mult_done, 6 * b + (2 * n + half - 1))
                    if n == 0 and half == 1:
                        pe.wait_ge(misc_used, nth(None if first else b - 1, "Z3") + 1)
                    three_passes(sc[:, half], lambda p: xT_p[:, k, p, ks * P:(ks + 1) * P],
                                 lambda p: z_p[:, p, 4 * half:4 * half + 4, qt * P:(qt + 1) * P]).then_inc(s_full, 1)

            def weigh(b, k, n, first, heads=range(H)):
                ks, qt = UNITS[n]
                m = (3 * k + n) % 2
                if 0 in heads:
                    if n == 0 and not first:
                        pe.wait_ge(ln_step, 4 * b - 3)
                    if n == 2:
                        pe.wait_ge(low_dve, b + 1)
                    else:
                        pe.wait_ge(low_pool, 2 * b + (n + 1))
                    pe.wait_ge(misc_used, nth(b, f"U{2 * ks + 1}") + 1)
                for h in heads:
                    for p, q in ((att_h, 0), (att_h, 1), (att_l, 0)):
                        mm = nc.tensor.matmul(acc[:, qt, :], p[:, m, h, :], u_p[:, q, ks, h * D:(h + 1) * D],
                                              start=(h == 0 and n < 2 and p is att_h and q == 0), stop=(h == H - 1 and n != 1 and p is att_l))
                if H - 1 in heads:
                    mm.then_inc(av_done, 1)

            def body(b, k, first=False, left=NB, seam=False):
                c, kn = b + 1, 1 - k
                rest = not (first or seam)
                arguments(b, k, 0, first)
                scores(b, k, 0, first)
                if rest:
                    weigh(b - 1, kn, 2, False, range(H // 2))
                arguments(b, k, 1, first)
                scores(b, k, 1, first)
                if rest:
                    weigh(b - 1, kn, 2, False, range(H // 2, H))
                r_u(b, k, (0, 1))
                if left >= 1:
                    r_gt(b, c)
                arguments(b, k, 2, first)
                scores(b, k, 2, first)
                r_u(b, k, (2, 3))
                if left >= 2:
                    r_turn(b, "T", b + 2)
                weigh(b, k, 0, first, range(H // 2))
                if left >= 1:
                    r_z(b, kn, (0,))
                weigh(b, k, 0, first, range(H // 2, H))
                if left >= 1:
                    r_z(b, kn, (1,))
                weigh(b, k, 1, first, range(H // 2))
                if left >= 1:
                    r_z(b, kn, (2,))
                    r_v(b, c, range(3))
                    r_z(b, kn, (3,))
                    r_v(b, c, (3,))
                weigh(b, k, 1, first, range(H // 2, H))
                if left >= 2:
                    r_logits(b, "DL", k, "T")

            def experts():
                def expert_of(n, k):
                    return nc.tensor.value_load(texpi[0:1, bass.ds(k, 1)], min_val=0, max_val=E - 1)

                def turn_rows(k, q):
                    pe.wait_ge(xf_done, k + 1)
                    nc.tensor.transpose(sc[:, q % 2, 0, :], xf[:, q % 2, :], ident[:]).then_inc(xT_full, 1)

                def hidden(k, q):
                    e = expert_of(0, k)
                    pe.wait_ge(xT_done, k + 1)
                    pe.wait_ge(sel_done, k + 1)
                    nc.tensor.matmul(arg_bank[q % 2], sel[:, q, :], bparts[:, 0:F], start=True, stop=False)
                    nc.tensor.matmul(arg_bank[q % 2], xfT[:, q % 2, :], w1[:, bass.ds(e, 1), :].rearrange("p a f -> p (a f)"),
                                     start=False, stop=True).then_inc(h_full, 1)

                def turn_hidden(k, q):
                    pe.wait_ge(h_done, k + 1)
                    for t in range(FT):
                        mm = nc.tensor.transpose(misc[:, q % 2, t * P:(t + 1) * P], hb[:, q % 2, t * P:(t + 1) * P], ident[:])
                    mm.then_inc(hT_full, 1)

                def project(k, q):
                    e = expert_of(1, k)
                    pe.wait_ge(hT_done, k + 1)
                    if not (isinstance(k, int) and k < 2):
                        pe.wait_ge(yx_done, k - 1)
                    nc.tensor.matmul(ybank[q % 2], sel[:, q, :], bparts[:, F:F + D], start=True, stop=False)
                    for t in range(FT):
                        mm = nc.tensor.matmul(ybank[q % 2], hT[:, q % 2, t * P:(t + 1) * P],
                                              w2[:, bass.ds(e, 1), t, :].rearrange("p a d -> p (a d)"), start=False, stop=(t == FT - 1))
                    mm.then_inc(yx_full, 1)

                weigh(HALF - 1, 1, 2, False)
                pe.wait_ge(w1_ready, 1)
                pe.wait_ge(misc_used, nth(HALF - 1, "DL") + 1)
                pe.wait_ge(mult_done, 6 * HALF)
                staggered(((2, turn_rows), (1, hidden), (0, turn_hidden), (-1, project)), pe)
                pe.wait_ge(yx_done, ST)

            pe.wait_ge(w_in, W_IN)
            pe.wait_ge(gate_ready, 1)
            router(range(0, 3 * NG // 4))
            mn_products()
            router(range(3 * NG // 4, NG))
            pe.wait_ge(mn_used, 4)
            r_turn(None, "T0", 0)
            r_logits(None, "DL0", 0, "T0")
            ranks()
            r_z(None, 0, range(4))
            r_turn(None, "T1", 1)
            r_gt(None, 0)
            r_v(None, 0)
            r_logits(None, "DL1", 1, "T1")
            pe.wait_ge(sorted_, 1)
            body(0, 0, first=True)
            body(1, 1)
            with pe.Fori(1, HALF // 2) as i:
                body(2 * i, 0)
                body(2 * i + 1, 1)
            experts()
            body(HALF, 0, seam=True)
            body(HALF + 1, 1)
            with pe.Fori(HALF // 2 + 1, NB // 2 - 1) as i:
                body(2 * i, 0)
                body(2 * i + 1, 1)
            body(NB - 2, 0, left=1)
            body(NB - 1, 1, left=0)
            weigh(NB - 1, 1, 2, False)

        @block.scalar
        def _(act):
            nc.scalar.preload_act_table_set("natural_log_exp_and_others")
            act.wait_ge(const_set, CONSTS)

            def high(b, r, dst, src):
                act.wait_ge(misc_full, nth(b, r) + 1)
                nc.scalar.copy(dst, src).then_inc(high_done, 1)

            def square(c):
                act.wait_ge(chunk_step, 3 * c + 3)
                if c:
                    act.wait_ge(ssq_done, c)
                nc.scalar.activation(squares, xn_all[:, c * XC:(c + 1) * XC, 0:D], ACT.Square).then_inc(sq_done, 1)

            def spread(c):
                act.wait_ge(ssq_done, c + 1)
                t = slice(c * XC, (c + 1) * XC)
                nc.scalar.activation(lnv[:, t], dev[:, t], ACT.Ln, bias=consts[:, 0:1], scale=1.0 / D).then_inc(rstd_step, 1)
                act.wait_ge(rstd_step, c + 1)
                nc.scalar.activation(rstd[:, t], lnv[:, t], ACT.Exp, scale=-0.5).then_inc(rstd_done, 1)

            def turned_out(c):
                for j in range(c * NG // 4, (c + 1) * NG // 4):
                    act.wait_ge(turned, j + 1)
                    if j >= 2:
                        act.wait_ge(logit_full, j - 1)
                    nc.scalar.copy(stageT[j % 2], arg_bank[j % 2]).then_inc(unturned, 1)

            square(0)
            spread(0)
            square(1)
            spread(1)
            square(2)
            turned_out(0)
            spread(2)
            square(3)
            turned_out(1)
            spread(3)
            turned_out(2)
            for k in range(2):
                act.wait_ge(mn_full, 3 + k)
                nc.scalar.copy(n_p[:, 0, 512 * k:512 * k + 512], misc[:, 1 + k, :]).then_inc(n_high, 1)
            turned_out(3)
            act.wait_ge(rr_step, 2)
            nc.scalar.activation(lnv[:], msq[:], ACT.Ln, bias=consts[:, 3:4], scale=1.0 / D).then_inc(rr_step, 1)
            act.wait_ge(rr_step, 3)
            nc.scalar.activation(xn_all[:, :, C_RMS], lnv[:], ACT.Exp, scale=-0.5).then_inc(rr_done, 1)

            def turn(b, r, k):
                high(b, r, xT_p[:, k, 0, :], misc[:, bank(b, r), 0:T])

            def logits(b, r):
                act.wait_ge(misc_full, nth(b, r) + 1)
                for g in range(2):
                    nc.scalar.activation(zz[:, g, :], misc[0:VC, bank(b, r), g * T:(g + 1) * T], ACT.Identity,
                                         bias=zbias[:, g:g + 1]).then_inc(zz_done, 1)

            def softlog(b, r, c):
                act.wait_ge(misc_used, nth(b, r) + 1)
                nc.scalar.activation(na[:], na[:], ACT.Exp).then_inc(ex_done, 1)
                act.wait_ge(ex_done, c + 1)
                nc.scalar.activation(na[:], na[:], ACT.Ln, bias=consts[0:VC, 1:2]).then_inc(l1_done, 1)

            def loglam(c):
                act.wait_ge(sp_done, c + 1)
                nc.scalar.activation(lnlam[:], zz[:, 0, :], ACT.Ln, bias=consts[0:VC, 2:3]).then_inc(lnlam_done, 1)

            def z_out(b, part):
                for n in part:
                    high(b, f"Z{n}", z_p[:, 0, 2 * n:2 * n + 2, :], misc[:, bank(b, f"Z{n}"), :].rearrange("p (h t) -> p h t", h=2))

            def u_out(b, part):
                for n in part:
                    high(b, f"U{n}", u_p[:, 0, n // 2, (n % 2) * 512:(n % 2 + 1) * 512], misc[:, bank(b, f"U{n}"), :])

            def exps(b, k, n, first):
                ks, qt = UNITS[n]
                m = (3 * k + n) % 2
                act.wait_ge(arg_full, 3 * b + (n + 1))
                if not (first and n < 2):
                    act.wait_ge(mult_done, 6 * b + (2 * n - 2))
                for h in range(H):
                    ins = nc.scalar.activation(expo[:, m, h, :].rearrange("p (a c) -> p a c", a=2), arg[:, :, h, :], ACT.Exp,
                                               bias=negG[:, k, ks, h:h + 1])
                ins.then_inc(exp_done, 1)

            def att_out(b, k, n, first):
                m = (3 * k + n) % 2
                act.wait_ge(mult_done, 6 * b + (2 * n + 2))
                if not (first and n < 2):
                    act.wait_ge(av_done, 3 * b + (n - 1))
                nc.scalar.copy(att_h[:, m], att[:, m]).then_inc(att_high, 1)

            def out_rstd(b):
                act.wait_ge(ostat_done, b + 1)
                nc.scalar.activation(orstd[:], odev[:], ACT.Ln, bias=consts[:, 0:1], scale=1.0 / D).then_inc(olog_done, 1)
                act.wait_ge(olog_done, b + 1)
                nc.scalar.activation(orstd[:], orstd[:], ACT.Exp, scale=-0.5).then_inc(orstd_done, 1)

            def body(b, k, first=False, left=NB):
                c, kn = b + 1, 1 - k
                exps(b, k, 0, first)
                if left >= 1:
                    softlog(None if first else b - 1, "DL1" if first else "DL", c)
                exps(b, k, 1, first)
                att_out(b, k, 0, first)
                if left >= 1:
                    loglam(c)
                u_out(b, (0,))
                exps(b, k, 2, first)
                u_out(b, (1,))
                att_out(b, k, 1, first)
                if not first:
                    out_rstd(b - 1)
                u_out(b, (2, 3))
                if left >= 2:
                    turn(b, "T", k)
                if left >= 1:
                    z_out(b, (0, 1))
                att_out(b, k, 2, first)
                if left >= 1:
                    z_out(b, (2, 3))
                if left >= 2:
                    logits(b, "DL")

            def experts():
                def rows_turned(k, q):
                    act.wait_ge(xT_full, k + 1)
                    if not (isinstance(k, int) and k < 2):
                        act.wait_ge(h_full, k - 1)
                    nc.scalar.copy(xfT[:, q % 2, :], sc[:, q % 2, 0, :]).then_inc(xT_done, 1)

                def silu(k, q):
                    act.wait_ge(h_full, k + 1)
                    if not (isinstance(k, int) and k < 2):
                        act.wait_ge(hT_full, k - 1)
                    nc.scalar.activation(hb[:, q % 2, :], arg_bank[q % 2], ACT.Silu).then_inc(h_done, 1)

                nc.scalar.preload_act_table_set("silu_and_others")
                staggered(((2, rows_turned), (1, silu)), act)
                nc.scalar.preload_act_table_set("natural_log_exp_and_others")

            turn(None, "T0", 0)
            logits(None, "DL0")
            softlog(None, "DL0", 0)
            act.wait_ge(sort_step, 4)
            nc.scalar.activation(grid[1], grid[1], ACT.Exp).then_inc(score_exp, 1)
            loglam(0)
            z_out(None, range(4))
            turn(None, "T1", 1)
            logits(None, "DL1")
            act.wait_ge(sorted_, 1)
            body(0, 0, first=True)
            body(1, 1)
            with act.Fori(1, HALF // 2) as i:
                body(2 * i, 0)
                body(2 * i + 1, 1)
            experts()
            with act.Fori(HALF // 2, NB // 2 - 1) as i:
                body(2 * i, 0)
                body(2 * i + 1, 1)
            body(NB - 2, 0, left=1)
            body(NB - 1, 1, left=0)
            out_rstd(NB - 1)

        def as_f32(ap):
            return ap.bitcast(F32)

        @block.vector
        def _(dve):
            nc.vector.memset(rowst[:, 0, :], 0.0).then_inc(zero_set, 1)
            fills = [(consts[:, 0:1], 1e-5), (consts[:, 1:2], 1.0), (consts[:, 2:3], LAM_MIN), (consts[:, 3:4], 1e-6), (ones[:], 1.0),
                     (ones128[:], 1.0), (idle0[:], 0.0), (xn_all[:, :, D:XW], 0.0)]
            assert len(fills) == CONSTS
            for dst, v in fills:
                nc.vector.memset(dst, v).then_inc(const_set, 1)

            def col(t, c):
                return t[:, c * XC:(c + 1) * XC].rearrange("p (t a) -> p t a", a=1).broadcast_to([P, XC, D])

            def centre(c):
                xc = xn_all[:, c * XC:(c + 1) * XC, 0:D]
                t = slice(c * XC, (c + 1) * XC)
                dve.wait_ge(x_in[c], 16)
                nc.vector.tensor_reduce(ssum[:, t], xc, AX_X, ALU.add).then_inc(chunk_step, 1)
                dve.wait_ge(chunk_step, 3 * c + 1)
                nc.vector.tensor_scalar(mean[:, t], ssum[:, t], 1.0 / D, None, ALU.mult).then_inc(chunk_step, 1)
                dve.wait_ge(chunk_step, 3 * c + 2)
                nc.vector.tensor_tensor(xc, xc, col(mean, c), ALU.subtract).then_inc(chunk_step, 1)

            def deviation(c):
                dve.wait_ge(sq_done, c + 1)
                nc.vector.tensor_reduce(dev[:, c * XC:(c + 1) * XC], squares.rearrange("p (t d) -> p t d", d=D), AX_X,
                                        ALU.add).then_inc(ssq_done, 1)

            def scale(c):
                xc = xn_all[:, c * XC:(c + 1) * XC, 0:D]
                dve.wait_ge(rstd_done, c + 1)
                nc.vector.tensor_tensor(xc, xc, col(rstd, c), ALU.mult).then_inc(xn_done, 1)

            centre(0)
            centre(1)
            deviation(0)
            centre(2)
            deviation(1)
            scale(0)
            centre(3)
            deviation(2)
            scale(1)
            deviation(3)
            scale(2)
            scale(3)
            nc.vector.tensor_tensor(msq[:], dev[:], rstd[:], ALU.mult).then_inc(rr_step, 1)
            dve.wait_ge(rr_step, 1)
            nc.vector.tensor_tensor(msq[:], msq[:], rstd[:], ALU.mult).then_inc(rr_step, 1)

            dve.wait_ge(w_in, W_IN)
            nc.vector.tensor_copy(wlog_p[:, 0, :], wlog[:]).then_inc(wlog_step, 1)
            dve.wait_ge(wlog_step, 1)
            nc.vector.tensor_tensor(wlog_p[:, 1, :], wlog[:], as_f32(wlog_p[:, 0, :]), ALU.subtract).then_inc(wlog_step, 1)
            for k in range(2):
                dve.wait_ge(mn_full, 1 + k)
                hi, lo = m_p[:, 0, 4 * k:4 * k + 4, :], m_p[:, 1, 4 * k:4 * k + 4, :]
                nc.vector.tensor_scalar(hi, sc[:, k], float(D) ** -0.5, None, ALU.mult).then_inc(mn_step, 1)
                dve.wait_ge(mn_step, k + 1)
                nc.vector.scalar_tensor_tensor(out=lo, in0=sc[:, k], scalar=float(D) ** -0.5, in1=as_f32(hi), op0=ALU.mult,
                                               op1=ALU.subtract).then_inc(mn_used, 1)
            for k in range(2):
                dve.wait_ge(n_high, k + 1)
                at = slice(512 * k, 512 * k + 512)
                nc.vector.tensor_tensor(n_p[:, 1, at], misc[:, 1 + k, :], as_f32(n_p[:, 0, at]), ALU.subtract).then_inc(mn_used, 1)

            def low(b, r, dst, src, hi):
                dve.wait_ge(high_done, nth_cut(b, r) + 1)
                nc.vector.tensor_tensor(dst, src, as_f32(hi), ALU.subtract).then_inc(misc_used, 1)

            def turn(b, r, k):
                low(b, r, xT_p[:, k, 1, :], misc[:, bank(b, r), 0:T], xT_p[:, k, 0, :])

            def z_out(b, part):
                for n in part:
                    low(b, f"Z{n}", z_p[:, 1, 2 * n:2 * n + 2, :], misc[:, bank(b, f"Z{n}"), :].rearrange("p (h t) -> p h t", h=2),
                        z_p[:, 0, 2 * n:2 * n + 2, :])

            def u_out(b, part):
                for n in part:
                    at = slice((n % 2) * 512, (n % 2 + 1) * 512)
                    low(b, f"U{n}", u_p[:, 1, n // 2, at], misc[:, bank(b, f"U{n}"), :], u_p[:, 0, n // 2, at])

            def minus_abs(c):
                dve.wait_ge(zz_done, 2 * c + 2)
                nc.vector.scalar_tensor_tensor(out=na[:], in0=zz[:], scalar=-1.0, in1=zz[:], op0=ALU.mult, op1=ALU.min).then_inc(misc_used, 1)

            def softplus_scan(c):
                dve.wait_ge(l1_done, c + 1)
                nc.vector.scalar_tensor_tensor(out=zz[:], in0=zz[:], scalar=0.0, in1=na[:], op0=ALU.max, op1=ALU.add).then_inc(sp_done, 1)
                dve.wait_ge(sp_done, c + 1)
                nc.vector.tensor_tensor_scan(gsum[:], ones[:], zz[:, 1, :], 0.0, ALU.mult, ALU.subtract).then_inc(scan_done, 1)

            def parts(c, first=False):
                dve.wait_ge(lnlam_done, c + 1)
                dve.wait_ge(scan_done, c + 1)
                nc.vector.tensor_tensor(v32[:], lnlam[:], gsum[:], ALU.add).then_inc(part_step, 1)
                if not first:
                    dve.wait_ge(vrows, NP3 * 2 * 16 * c)
                dve.wait_ge(part_step, 4 * c + 1)
                nc.vector.tensor_copy(p3[:, 0, :], v32[:]).then_inc(part_step, 1)
                dve.wait_ge(part_step, 4 * c + 2)
                nc.vector.tensor_tensor(v32[:], v32[:], p3[:, 0, :], ALU.subtract).then_inc(part_step, 1)
                dve.wait_ge(part_step, 4 * c + 3)
                nc.vector.tensor_copy(p3[:, 1, :], v32[:]).then_inc(part_step, 1)
                dve.wait_ge(part_step, 4 * c + 4)
                nc.vector.tensor_tensor(p3[:, 2, :], v32[:], p3[:, 1, :], ALU.subtract).then_inc(parts_done, 1)

            def gates_out(b, k):
                dve.wait_ge(misc_full, nth(b, "GT") + 1)
                src = misc[:, bank(b, "GT"), 0:2 * VC].rearrange("p (a h l) -> p a h l", a=2, l=LV)[:, :, :, 0]
                nc.vector.tensor_scalar(negG[:, k], src, -1.0, None, ALU.mult).then_inc(misc_used, 1)

            def values_out(b, part=range(4)):
                for n in part:
                    r = f"V{n}"
                    dve.wait_ge(misc_full, nth(b, r) + 1)
                    nc.vector.tensor_tensor(val[0:VR, 2 * n:2 * n + 2, :], misc[0:VR, bank(b, r), :].rearrange("p (h t) -> p h t", h=2),
                                            own[:].rearrange("p (a t) -> p a t", a=1).broadcast_to([VR, 2, T]), ALU.mult).then_inc(misc_used, 1)

            def products(b, k, n, first):
                m = (3 * k + n) % 2
                dve.wait_ge(exp_done, 3 * b + (n + 1))
                if n == 0 and not first:
                    dve.wait_ge(low_pool, 2 * b)
                if n == 2:
                    dve.wait_ge(low_pool, 2 * b + 1)
                for half in range(2):
                    dve.wait_ge(s_full, 6 * b + (2 * n + half + 1))
                    nc.vector.tensor_tensor(att[:, m, 4 * half:4 * half + 4, :], sc[:, half], expo[:, m, 4 * half:4 * half + 4, :],
                                            ALU.mult).then_inc(mult_done, 1)

            def att_low(b, k):
                m = (3 * k + 2) % 2
                dve.wait_ge(att_high, 3 * b + 3)
                nc.vector.tensor_tensor(att_l[:, m], att[:, m], as_f32(att_h[:, m]), ALU.subtract).then_inc(low_dve, 1)

            def moments(st, total, diff, mu, dv, done, c):
                nc.vector.tensor_tensor(diff[:], st[:, :, 1], st[:, :, 4], ALU.subtract).then_inc(done, 1)
                nc.vector.tensor_tensor(total[:], st[:, :, 1:3], st[:, :, 4:6], ALU.add).then_inc(done, 1)
                dve.wait_ge(done, c + 2)
                nc.vector.tensor_tensor(diff[:], diff[:], diff[:], ALU.mult).then_inc(done, 1)
                nc.vector.tensor_scalar(mu[:], total[:, :, 0], 0.5, None, ALU.mult).then_inc(done, 1)
                dve.wait_ge(done, c + 4)
                return nc.vector.scalar_tensor_tensor(out=dv[:], in0=diff[:], scalar=D / 4.0, in1=total[:, :, 1], op0=ALU.mult, op1=ALU.add)

            def statistics(b):
                dve.wait_ge(av_done, 3 * b + 3)
                nc.vector.tensor_tensor(o[:], acc[:, 0:2, :], xn_all[:, bass.ds(2 * b, 2), 0:D], ALU.add).then_inc(ln_step, 1)
                dve.wait_ge(ln_step, 4 * b + 1)
                for n in range(2):
                    nc.vector.bn_stats(ostats[:, n, :], o[:, n, :]).then_inc(ln_step, 1)
                dve.wait_ge(ln_step, 4 * b + 3)
                moments(ostats, osum, odif, omean, odev, omom_step, 4 * b).then_inc(ostat_done, 1)

            def normalise(b):
                if not (isinstance(b, int) and b == 0):
                    dve.wait_ge(y_step, 3 * b)
                dve.wait_ge(orstd_done, b + 1)
                nc.vector.tensor_scalar(y[:, 0, :], o[:, 0, :], omean[:, 0:1], orstd[:, 0:1], ALU.subtract, ALU.mult).then_inc(ln_step, 1)
                nc.vector.tensor_scalar(y[:, 1, :], o[:, 1, :], omean[:, 1:2], orstd[:, 1:2], ALU.subtract, ALU.mult).then_inc(y_done, 1)

            def body(b, k, first=False, left=NB):
                c, kn = b + 1, 1 - k
                products(b, k, 0, first)
                if left >= 1:
                    softplus_scan(c)
                if not first:
                    statistics(b - 1)
                products(b, k, 1, first)
                u_out(b, (0,))
                if left >= 1:
                    parts(c)
                u_out(b, (1,))
                if left >= 1:
                    gates_out(b, kn)
                products(b, k, 2, first)
                u_out(b, (2, 3))
                if left >= 2:
                    turn(b, "T", k)
                if not first:
                    normalise(b - 1)
                if left >= 1:
                    z_out(b, range(3))
                    values_out(b, range(3))
                    z_out(b, (3,))
                    values_out(b, (3,))
                att_low(b, k)
                if left >= 2:
                    minus_abs(b + 2)

            def sort():
                count = [0]

                def then(ins):
                    count[0] += 1
                    ins.then_inc(sort_step, 1)
                    dve.wait_ge(sort_step, count[0])

                def te(x):
                    return x.rearrange("p (t e) -> p t e", e=E)

                def over_e(col):
                    return col.rearrange("p (t a) -> p t a", a=1).broadcast_to([P, NT, E])

                def over_t(row, n=NT):
                    return row.rearrange("p (a e) -> p a e", a=1).broadcast_to([P, n, E])

                logit, gap, low, oh, pos, carry = grid[0], grid[1], grid[2], grid[3], grid[4], grid[5]
                top, expert = small64[:, 0, :], small64[:, 1, :]
                total, tiles, ends, starts = small[:, 0], small[:, 1], small[:, 2], small[:, 3]
                dve.wait_ge(logit_full, NG)
                dve.wait_ge(rr_done, 1)
                rms = xn_all[:, :, C_RMS:C_RMS + 1].broadcast_to([P, NT, E])
                then(nc.vector.tensor_tensor(te(logit), te(acc[:].rearrange("p a d -> p (a d)")), rms, ALU.mult))
                then(nc.vector.tensor_reduce(top, te(logit), AX_X, ALU.max))
                then(nc.vector.tensor_tensor(te(gap), te(logit), over_e(top), ALU.subtract))
                then(nc.vector.tensor_scalar(low, gap, 0.0, float(E), ALU.is_lt, ALU.mult))
                then(nc.vector.tensor_tensor(te(low), te(low), over_t(eid[:]), ALU.add))
                then(nc.vector.tensor_reduce(expert, te(low), AX_X, ALU.min))
                then(nc.vector.tensor_tensor(te(oh), over_t(eid[:]), over_e(expert), ALU.is_equal))
                nc.vector.tensor_copy(onehot, oh).then_inc(onehot_done, 1)
                dve.wait_ge(score_exp, 1)
                then(nc.vector.tensor_reduce(top, te(gap), AX_X, ALU.add))
                then(nc.vector.reciprocal(xn_all[:, :, C_SCORE], top))
                yield
                dve.wait_ge(rank_full, 1)
                then(nc.vector.tensor_copy(pos, arg_bank[1]))
                for e in range(E):
                    ins = nc.vector.tensor_tensor_scan(te(carry)[:, :, e], ones128[:, 0:NT], te(pos)[:, :, e], 0.0, ALU.mult, ALU.add)
                    if e < E - 1:
                        ins.then_inc(sort_step, 1)
                        count[0] += 1
                then(ins)
                nc.vector.tensor_copy(total, te(carry)[:, NT - 1, :]).then_inc(sort_step, 1)
                count[0] += 1
                then(nc.vector.tensor_tensor(pos, carry, pos, ALU.subtract))
                kp = kP[:].rearrange("p (a t) -> p a t", a=1).broadcast_to([P, E, NT])
                many = total.rearrange("p (e a) -> p e a", a=1).broadcast_to([P, E, NT])
                g7 = grid[7].rearrange("p (e t) -> p e t", e=E)
                then(nc.vector.tensor_tensor(g7, many, kp, ALU.is_gt))
                then(nc.vector.tensor_reduce(tiles, g7, AX_X, ALU.add))
                then(nc.vector.tensor_tensor_scan(ends, ones128[:, 0:E], tiles, 0.0, ALU.mult, ALU.add))
                then(nc.vector.tensor_tensor(starts, ends, tiles, ALU.subtract))
                then(nc.vector.tensor_scalar(starts, starts, float(P), None, ALU.mult))
                then(nc.vector.tensor_tensor(te(pos), te(pos), over_t(starts), ALU.add))
                then(nc.vector.tensor_tensor(pos, pos, arg_bank[0], ALU.add))
                then(nc.vector.tensor_tensor(pos, pos, oh, ALU.mult))
                then(nc.vector.tensor_reduce(expert, te(pos), AX_X, ALU.add))
                then(nc.vector.tensor_copy(slot[:], expert))
                tg = tgrid.rearrange("p (t e) -> p t e", e=E)
                tid = tileid[:].rearrange("p (t a) -> p t a", a=1).broadcast_to([P, ST, E])
                then(nc.vector.tensor_tensor(tg, over_t(ends, ST), tid, ALU.is_le))
                then(nc.vector.tensor_reduce(texp[:], tg, AX_X, ALU.add))
                then(nc.vector.tensor_scalar(texp[:], texp[:], float(E - 1), None, ALU.min))
                then(nc.vector.tensor_scalar(tsel[:], texp[0:NP3 * E, :], prow[:, 0:1], None, ALU.is_equal))
                nc.vector.tensor_copy(texpi[:], texp[0:1, :]).then_inc(sorted_, 1)

            def experts():
                def scale_rows(k, q):
                    dve.wait_ge(xs_in[q], 16 * ((k - q) // NS) + 16 if isinstance(k, int) else 4 * (k - q) + 16)
                    if not (isinstance(k, int) and k < 2):
                        dve.wait_ge(xT_full, k - 1)
                    nc.vector.tensor_scalar(xf[:, q % 2, :], xs[:, q, 0:D], xs[:, q, C_RMS:C_RMS + 1], None, ALU.mult).then_inc(xf_done, 1)

                def select(k, q):
                    if not (isinstance(k, int) and k < NS):
                        dve.wait_ge(yx_full, k - 3)
                    nc.vector.tensor_scalar(sel[:, q, :], ones128[0:NP3 * E, :], tsel[:, bass.ds(k, 1)], None, ALU.mult).then_inc(sel_done, 1)

                def hidden_turned(k, q):
                    dve.wait_ge(hT_full, k + 1)
                    if not (isinstance(k, int) and k < 2):
                        dve.wait_ge(yx_full, k - 1)
                    nc.vector.tensor_copy(hT[:, q % 2, :], misc[:, q % 2, :]).then_inc(hT_done, 1)

                def output(k, q):
                    dve.wait_ge(yx_full, k + 1)
                    if not (isinstance(k, int) and k < NS):
                        dve.wait_ge(y_out[q], 16 * ((k - q) // NS) if isinstance(k, int) else 4 * (k - q))
                    nc.vector.tensor_copy(yb[:, q, :], ybank[q % 2]).then_inc(yx_done, 1)

                staggered(((3, scale_rows), (2, select), (0, hidden_turned), (-1, output)), dve)

            turn(None, "T0", 0)
            minus_abs(0)
            sorting = sort()
            next(sorting)
            softplus_scan(0)
            parts(0, True)
            z_out(None, range(4))
            turn(None, "T1", 1)
            for _ in sorting:
                pass
            gates_out(None, 0)
            values_out(None)
            minus_abs(1)
            body(0, 0, first=True)
            body(1, 1)
            with dve.Fori(1, HALF // 2) as i:
                body(2 * i, 0)
                body(2 * i + 1, 1)
            experts()
            with dve.Fori(HALF // 2, NB // 2 - 1) as i:
                body(2 * i, 0)
                body(2 * i + 1, 1)
            body(NB - 2, 0, left=1)
            body(NB - 1, 1, left=0)
            statistics(NB - 1)
            normalise(NB - 1)

        @block.gpsimd
        def _(pool):
            def pair(t):
                return t[:].rearrange("p (a d) -> p a d", a=1).broadcast_to([P, 2, D])

            def stage_x(b):
                nc.gpsimd.tensor_copy(xnb[:], xn_all[:, bass.ds(2 * b, 2), 0:D]).then_inc(xnb_done, 1)

            def att_low(b, k, n):
                m = (3 * k + n) % 2
                pool.wait_ge(att_high, 3 * b + (n + 1))
                nc.gpsimd.tensor_tensor(att_l[:, m], att[:, m], as_f32(att_h[:, m]), ALU.subtract).then_inc(low_pool, 1)

            def carry_wait():
                nc.gpsimd.tensor_tensor(idle[:], idle0[:], idle0[:], ALU.add)

            def send_rows(b, first):
                if not first:
                    for q in range(4):
                        pool.wait_ge(row_out[q], 16 * b)
                nc.gpsimd.tensor_copy(slotst[:], slot[:, bass.ds(4 * b, 4)]).then_inc(row_copy, 1)
                nc.gpsimd.tensor_copy(rowst[:], xn_all[:, bass.ds(4 * b, 4), :]).then_inc(row_copy, 1)
                pool.wait_ge(row_copy, 2 * b + 2)
                carry_wait()
                for q in range(4):
                    nc.gpsimd.indirect_dma_start(out=rows_dram, out_offset=bass.IndirectOffsetOnAxis(ap=slotst[:, q:q + 1], axis=0),
                                                 in_=rowst[:, q, :], in_offset=None).then_inc(row_out[q], 16)

            def fetch_rows(b):
                nc.gpsimd.tensor_copy(slotst[:, 0:2], slot[:, bass.ds(2 * b, 2)]).then_inc(slot_copy, 1)
                nc.gpsimd.tensor_copy(slotst[:, 2:4], slot[:, bass.ds(2 * b - NB, 2)]).then_inc(slot_copy, 1)
                pool.wait_ge(slot_copy, 2 * b - (NB - 2))
                carry_wait()
                for q in range(4):
                    nc.gpsimd.indirect_dma_start(out=got[:, q, :], out_offset=None, in_=y_dram,
                                                 in_offset=bass.IndirectOffsetOnAxis(ap=slotst[:, q:q + 1], axis=0)).then_inc(got_in[q], 16)

            def finish(b, i, k, half):
                pool.wait_ge(y_done, b + 1)
                pool.wait_ge(ln_step, 4 * b + 4)
                nc.gpsimd.tensor_tensor(y[:], y[:], pair(lng), ALU.mult).then_inc(y_step, 1)
                pool.wait_ge(y_step, 3 * b + 1)
                nc.gpsimd.tensor_tensor(y[:], y[:], pair(lnb), ALU.add).then_inc(y_step, 1)
                pool.wait_ge(base_in[k], 32 * i + 32)
                pool.wait_ge(y_step, 3 * b + 2)
                nc.gpsimd.tensor_tensor(base[:, k, 0:2, :], base[:, k, 0:2, :], y[:], ALU.add).then_inc(y_step, 1)
                if half:
                    for q in range(4):
                        pool.wait_ge(got_in[q], 16 * b - 16 * (HALF - 1))
                    for n, t in ((0, 2 * b), (1, 2 * b - NB)):
                        score = xn_all[:, bass.ds(t, 2), C_SCORE:C_SCORE + 1].broadcast_to([P, 2, D])
                        nc.gpsimd.tensor_tensor(got[:, 2 * n:2 * n + 2, :], got[:, 2 * n:2 * n + 2, :], score, ALU.mult).then_inc(scored, 1)
                    pool.wait_ge(y_step, 3 * b + 3)
                    for n in range(2):
                        pool.wait_ge(scored, 2 * b - (NB - n - 1))
                        part = base[:, k, 2 * n:2 * n + 2, :]
                        nc.gpsimd.tensor_tensor(part, part, got[:, 2 * n:2 * n + 2, :], ALU.add).then_inc(res_done, 1)

            def body(b, i, k, half, old_half, first=False, more=True):
                att_low(b, k, 0)
                att_low(b, k, 1)
                if more:
                    pool.wait_ge(misc_full, nth(b, "T") + 1)
                    stage_x(b + 3)
                if not first:
                    finish(b - 1, i - (1 - k), 1 - k, old_half)
                if not half:
                    send_rows(b, first)
                else:
                    if old_half:
                        pool.wait_ge(res_done, 2 * b - NB)
                    fetch_rows(b)

            pool.wait_ge(w_in, W_IN)
            bw = lambda c: prow[:, c:c + 1].broadcast_to([NP3 * E, F + D])
            pool.wait_ge(const_set, CONSTS)
            nc.gpsimd.tensor_scalar(gate[:], gate[:], rmsw[:, 0:1], None, ALU.mult).then_inc(gate_ready, 1)
            steps = [(bparts[:], bias32[:], None), (biasr, bparts[:], 1), (bias32[:], bias32[:], biasr), (bparts[:], bias32[:], None),
                     (biasr, bparts[:], 2), (bparts[:], bias32[:], biasr)]
            for n, (dst, src, by) in enumerate(steps):
                if by is None:
                    ins = nc.gpsimd.tensor_copy(dst, src)
                elif isinstance(by, int):
                    ins = nc.gpsimd.tensor_tensor(dst, src, bw(by), ALU.mult)
                else:
                    ins = nc.gpsimd.tensor_tensor(dst, src, by, ALU.add)
                ins.then_inc(bias_step, 1)
                pool.wait_ge(bias_step, n + 1)
            pool.wait_ge(xn_done, 1)
            stage_x(0)
            pool.wait_ge(w1_in, 16)
            nc.gpsimd.tensor_scalar(wstage[:].rearrange("p a b -> p (a b)"), wstage[:].rearrange("p a b -> p (a b)"), rmsw[:, 0:1], None,
                                    ALU.mult).then_inc(w1_ready, 1)
            for c in range(2):
                pool.wait_ge(misc_full, nth(None, f"T{c}") + 1)
                stage_x(c + 1)
            pool.wait_ge(sorted_, 1)
            pool.wait_ge(zeroed, 16)
            body(0, 0, 0, False, False, first=True)
            body(1, 0, 1, False, False)
            with pool.Fori(1, HALF // 2) as i:
                body(2 * i, i, 0, False, False)
                body(2 * i + 1, i, 1, False, False)
            for q in range(NS):
                pool.wait_ge(y_out[q], 16 * (ST // NS))
            body(HALF, HALF // 2, 0, True, False)
            body(HALF + 1, HALF // 2, 1, True, True)
            with pool.Fori(HALF // 2 + 1, NB // 2 - 2) as i:
                body(2 * i, i, 0, True, True)
                body(2 * i + 1, i, 1, True, True)
            body(NB - 4, NB // 2 - 2, 0, True, True)
            body(NB - 3, NB // 2 - 2, 1, True, True, more=False)
            body(NB - 2, NB // 2 - 1, 0, True, True, more=False)
            body(NB - 1, NB // 2 - 1, 1, True, True, more=False)
            finish(NB - 1, NB // 2 - 1, 1, True)


NAMES = ["x", "wlog", "zbias", "lng", "lnb", "w4", "c_level", "c_own", "c_causal", "c_rep", "c_ident",
         "gate", "rmsw", "bias", "w1", "w2", "c_before", "c_all", "c_eid", "c_kP", "c_tile", "c_prow"]


def kernel(**inputs):
    import numpy as _np
    import concourse.bacc as _bacc
    from concourse import mybir as _mybir
    from concourse.bass_utils import run_bass_kernel_spmd as _run

    g = {n: _np.asarray(v) for n, v in inputs.items()}
    wdl = g["L0_attn_Wdl"].reshape(H, 12, D)[:, :LV].reshape(VC, D)
    wgr = _np.repeat(g["L0_attn_Wg"], LV, axis=0)
    lp = g["L0_attn_Lparam"][:, :LV].reshape(VC)
    bg = _np.repeat(g["L0_attn_bg"], LV)
    by_head = lambda w: w.reshape(H, D, D).transpose(1, 0, 2).reshape(D, H * D)
    data = {
        "x": g["L0_attn_x"].reshape(NB * T, D),
        "wlog": _np.concatenate([wdl, wgr]).T, "zbias": _np.stack([lp, bg], 1),
        "lng": _np.tile(g["L0_attn_ln_g"][None], (P, 1)), "lnb": _np.tile(g["L0_attn_ln_b"][None], (P, 1)),
        "w4": _np.stack([by_head(g["L0_attn_Wq"]), by_head(g["L0_attn_Wk"]), by_head(g["L0_attn_Wv"]),
                         by_head(g["L0_attn_Wo"].T)]),
        "gate": g["L0_ffn_gate_w"].T, "rmsw": g["L0_ffn_rms_w"][:, None],
        "bias": _np.tile(_np.concatenate([g["L0_ffn_b1"], g["L0_ffn_b2"]], 1), (NP3, 1)),
        "w1": g["L0_ffn_W1"].transpose(1, 0, 2).reshape(D, E * F),
        "w2": g["L0_ffn_W2"].reshape(E, FT, P, D).transpose(2, 0, 1, 3).reshape(P, E * FT * D),
        **level_constants(),
    }
    nc = _bacc.Bacc("TRN2", target_bir_lowering=False, num_devices=1)
    arrays, args = {}, {}
    for name in NAMES:
        v = _np.ascontiguousarray(data[name])
        arrays[f"in_{name}"] = v
        args[name] = nc.dram_tensor(f"in_{name}", v.shape, _mybir.dt.from_np(v.dtype), kind="ExternalInput").ap()
    out = nc.dram_tensor("out_0", (NB * T, D), _mybir.dt.from_np(_np.dtype("float32")), kind="ExternalOutput").ap()
    build(nc, args, out)
    r = _run(nc, [arrays], core_ids=[0])
    return r.results[0]["out_0"].reshape(NB, T, D)
```

```python
from contextlib import ExitStack

import concourse.bass as bass
import numpy as np
from concourse import mybir

ALU = mybir.AluOpType
ACT = mybir.ActivationFunctionType
F32 = mybir.dt.float32
F32R = mybir.dt.float32r
I32 = mybir.dt.int32
U32 = mybir.dt.uint32
BF16 = mybir.dt.bfloat16
AX_X = mybir.AxisListType.X

P = 128
NB, T, D = 32, 256, 128
H = 8
LV = 9
TW = 4
NP3 = 3
HG = 4
VR = NP3 * TW * LV
CR = NP3 * HG * LV
KR = VR + TW
LW = T - TW + P
NT = NB * T // P
E, F = 8, 512
FT = F // P
BIG = -1.0e30
LAM_MIN = 2.0 ** -63
UNITS = [(0, 0), (0, 1), (1, 1)]
VC = H * LV
PREPARE = ["T0", "DL0", "Z0", "Z1", "Z2", "Z3", "T1", "GT", "V0", "V1", "V2", "V3", "DL1"]
BESIDE = ["U0", "U1", "U2", "U3", "GT", "T", "Z0", "Z1", "DL", "Z2", "Z3", "V0", "V1", "V2", "V3"]
BANKS = 3
HALF = NB // 2
XW = D + 4
C_RMS, C_SCORE = D, D + 1
ST = NT + E
GRP = 4
NG = NT // GRP
CONSTS = 8
NS = 4


def bf16_bits(a):
    return (np.ascontiguousarray(a, np.float32).view(np.uint32) >> 16).astype(np.uint16)


def level_constants():
    d = np.arange(TW)[:, None] - (np.arange(LW)[None, :] - (T - TW))
    lvl = np.where(d <= 0, 0, np.floor(np.log2(np.maximum(d, 1))).astype(int) + 1)
    m = np.zeros((KR, LW), np.float32)
    for p in range(NP3):
        for q in range(TW):
            for l in range(LV):
                m[(p * TW + q) * LV + l] = (d[q] >= 0) & (lvl[q] == l)
    m[VR:] = d < 0
    own = np.zeros((VR, T), np.float32)
    for r in range(VR):
        own[r] = np.arange(T) % TW == (r // LV) % TW
    causal = np.zeros((TW, H, T), np.float32)
    for q in range(TW):
        causal[q, :, q::TW] = BIG
    rep = np.zeros((CR, HG, VR), np.float32)
    for p in range(NP3):
        for h in range(HG):
            for q in range(TW):
                for l in range(LV):
                    rep[(p * HG + h) * LV + l, h, (p * TW + q) * LV + l] = 1
    return {
        "c_level": bf16_bits(m), "c_own": own, "c_causal": bf16_bits(causal.reshape(TW, H * T)),
        "c_before": bf16_bits(np.triu(np.ones((P, P), np.float32), 1)), "c_all": bf16_bits(np.ones((P, P), np.float32)),
        "c_eid": np.tile(np.arange(E, dtype=np.float32), (P, 1)), "c_kP": np.tile(P * np.arange(NT, dtype=np.float32), (P, 1)),
        "c_tile": np.tile(np.arange(ST, dtype=np.float32), (P, 1)),
        "c_prow": np.stack([np.arange(NP3 * E) % E, -1.0 * (np.arange(NP3 * E) >= E), -1.0 * (np.arange(NP3 * E) >= 2 * E)], 1).astype(np.float32),
        "c_rep": bf16_bits(rep.reshape(CR, HG * VR)), "c_ident": np.eye(P, dtype=np.float32),
    }


def build(nc, a, out):
    ctx = ExitStack()
    with ctx:
        def sb(name, shape, dt=F32):
            return ctx.enter_context(nc.sbuf_tensor(name, shape, dt))

        def psum(name, shape):
            return ctx.enter_context(nc.psum_tensor(name, shape, F32))

        def sem(name):
            return ctx.enter_context(nc.semaphore(name))

        level = sb("level", [KR, LW], BF16)
        own = sb("own", [VR, T])
        rep = sb("rep", [CR, HG, VR], BF16)
        ident = sb("ident", [P, P])
        before = sb("before", [P, P], BF16)
        allones = sb("allones", [P, P], BF16)
        eid = sb("eid", [P, E])
        kP = sb("kP", [P, NT])
        tileid = sb("tileid", [P, ST])
        prow = sb("prow", [NP3 * E, 3])
        ones128 = sb("ones128", [P, P])
        ones = sb("ones", [VC, T])
        consts = sb("consts", [P, 4])
        idle0 = sb("idle0", [1, 1])
        idle = sb("idle", [1, 1])
        wlog = sb("wlog", [P, 2 * VC])
        wlog_p = sb("wlog_p", [P, 2, 2 * VC], F32R)
        zbias = sb("zbias", [VC, 2])
        lng = sb("lng", [P, D])
        lnb = sb("lnb", [P, D])
        wstage = sb("wstage", [P, 4, H * D])
        w1 = wstage[:].rearrange("p a b -> p (a b)").rearrange("p (e f) -> p e f", e=E)
        w2 = sb("w2", [P, E, FT, D])
        m_p = sb("m_p", [P, 2, H, D], F32R)
        n_p = sb("n_p", [P, 2, H * D], F32R)
        gate = sb("gate", [P, E])
        rmsw = sb("rmsw", [P, 1])
        bparts = sb("bparts", [NP3 * E, F + D], BF16)
        xn_all = sb("xn_all", [P, NT, XW])
        ssum = sb("ssum", [P, NT])
        mean = sb("mean", [P, NT])
        dev = sb("dev", [P, NT])
        lnv = sb("lnv", [P, NT])
        rstd = sb("rstd", [P, NT])
        msq = sb("msq", [P, NT])
        slot = sb("slot", [P, NT], U32)
        texp = sb("texp", [P, ST])
        texpi = sb("texpi", [1, ST], I32)
        tsel = sb("tsel", [NP3 * E, ST])
        small = sb("small", [P, 8, E])
        small64 = sb("small64", [P, 2, NT])
        rowst = sb("rowst", [P, 4, XW])
        slotst = sb("slotst", [P, 4], U32)
        got = sb("got", [P, 4, D])
        base = sb("base", [P, 2, 4, D])
        xnb = sb("xnb", [P, 2, D])
        xT_p = sb("xT_p", [P, 2, 2, T], F32R)
        z_p = sb("z_p", [P, 2, H, T], F32R)
        u = sb("u", [P, 2, H * D])
        val = sb("val", [KR, H, T], BF16)
        negG = sb("negG", [P, 2, 2, H])
        zz = sb("zz", [VC, 2, T])
        na = sb("na", [VC, 2, T])
        gsum = sb("gsum", [VC, T])
        lnlam = sb("lnlam", [VC, T])
        v32 = sb("v32", [VC, T])
        p3 = sb("p3", [VC, NP3, T], BF16)
        vparts = sb("vparts", [CR, 2, T], BF16)
        expo = sb("expo", [P, 2, H, P])
        att = sb("att", [P, len(UNITS), H, P])
        o = sb("o", [P, 2, D])
        ostats = sb("ostats", [P, 2, 6])
        osum = sb("osum", [P, 2, 2])
        odif = sb("odif", [P, 2])
        omean = sb("omean", [P, 2])
        odev = sb("odev", [P, 2])
        orstd = sb("orstd", [P, 2])
        y = sb("y", [P, 2, D])

        eflat = expo[:].rearrange("p k h t -> p (k h t)")
        aflat = att[:].rearrange("p k h t -> p (k h t)")
        squares = eflat
        stageT = [aflat[:, 512 * k:512 * k + 512] for k in range(2)]
        grid = [(eflat, aflat)[k // 4][:, 512 * (k % 4):512 * (k % 4) + 512] for k in range(8)]
        onehot = grid[6][:, 0:NT * E // 2].bitcast(BF16)
        tgrid = eflat[:, 0:ST * E]
        bias32 = sb("bias32", [NP3 * E, F + D])
        biasr = sb("biasr", [NP3 * E, F + D])[:]
        xs = eflat[:, 0:NS * XW].rearrange("p (k d) -> p k d", k=NS)
        xf = eflat[:, 528:528 + 2 * D].rearrange("p (k d) -> p k d", k=2)
        hb = eflat[:, 1024:1024 + 2 * F].rearrange("p (k f) -> p k f", k=2)
        hT = aflat[:, 0:2 * F].rearrange("p (k f) -> p k f", k=2)
        xfT = aflat[:, 1024:1024 + 2 * D].rearrange("p (k d) -> p k d", k=2)
        sel = aflat[0:NP3 * E, 1280:1280 + NS * D // 2].bitcast(BF16).rearrange("p (k d) -> p k d", k=NS)
        yb = got

        misc = psum("misc", [P, BANKS, 512])
        arg = psum("arg", [P, 2, H, 64])
        sc = psum("sc", [P, 2, 4, P])
        acc = psum("acc", [P, 4, D])
        arg_bank = [arg[:, k].rearrange("p h t -> p (h t)") for k in range(2)]
        ybank = [acc[:, 2, :], misc[:, 2, 0:D]]

        def staggered(stages, eng):
            low, high = -3, ST + 1
            start, end = NS, (ST - NS) // NS * NS

            def step(k, q, static):
                for off, stage_ in stages:
                    if not static or 0 <= k + off < ST:
                        stage_(k + off, (q + off) % NS)

            for k in range(low, start):
                step(k, k % NS, True)
            with eng.Fori(start // NS, end // NS) as i:
                for q in range(NS):
                    step(NS * i + q, q, False)
            for k in range(end, high):
                step(k, k % NS, True)

        def rounds_of(b):
            if b is None:
                return PREPARE
            if isinstance(b, int) and b == NB - 1:
                return [r for r in BESIDE if r[0] == "U"]
            if isinstance(b, int) and b == NB - 2:
                return [r for r in BESIDE if r not in ("T", "DL")]
            return BESIDE

        def cut(rounds):
            return [r for r in rounds if r[0] in "TZ"]

        def count_before(b, full, prepare, short):
            if b is None:
                return 0
            return full * b + (prepare - (short if isinstance(b, int) and b == NB - 1 else 0))

        def nth(b, r):
            return count_before(b, len(BESIDE), len(PREPARE), 2) + rounds_of(b).index(r)

        def nth_cut(b, r):
            return count_before(b, len(cut(BESIDE)), len(cut(PREPARE)), 1) + cut(rounds_of(b)).index(r)

        def bank(b, r):
            shift = 2 if isinstance(b, int) and b == NB - 1 else 0
            return rounds_of(b).index(r) % BANKS if b is None else (len(PREPARE) - shift + rounds_of(b).index(r)) % BANKS

        assert len(BESIDE) % BANKS == 0

        w_in = sem("w_in")
        gate_in = sem("gate_in")
        wlog_in = sem("wlog_in")
        w2_in = sem("w2_in")
        wstage_in = sem("wstage_in")
        base_in0 = sem("base_in0")
        base_in1 = sem("base_in1")
        base_out0 = sem("base_out0")
        base_out1 = sem("base_out1")
        const_set = sem("const_set")
        bias_step = sem("bias_step")
        gate_ready = sem("gate_ready")
        chunk_step = sem("chunk_step")
        sq_done = sem("sq_done")
        ssq_done = sem("ssq_done")
        rstd_step = sem("rstd_step")
        rstd_done = sem("rstd_done")
        xn_done = sem("xn_done")
        rr_step = sem("rr_step")
        rr_done = sem("rr_done")
        turned = sem("turned")
        unturned = sem("unturned")
        logit_full = sem("logit_full")
        sort_step = sem("sort_step")
        score_exp = sem("score_exp")
        onehot_done = sem("onehot_done")
        rank_full = sem("rank_full")
        sorted_ = sem("sorted_")
        zero_set = sem("zero_set")
        zeroed = sem("zeroed")
        mn_full = sem("mn_full")
        n_high = sem("n_high")
        mn_step = sem("mn_step")
        mn_used = sem("mn_used")
        wlog_step = sem("wlog_step")
        w1_in = sem("w1_in")
        w1_ready = sem("w1_ready")
        xnb_done = sem("xnb_done")
        misc_full = sem("misc_full")
        high_done = sem("high_done")
        misc_used = sem("misc_used")
        zz_done = sem("zz_done")
        ex_done = sem("ex_done")
        l1_done = sem("l1_done")
        sp_done = sem("sp_done")
        lnlam_done = sem("lnlam_done")
        scan_done = sem("scan_done")
        part_step = sem("part_step")
        vrows = sem("vrows")
        arg_full = sem("arg_full")
        exp_done = sem("exp_done")
        s_full = sem("s_full")
        mult_done = sem("mult_done")
        av_done = sem("av_done")
        ln_step = sem("ln_step")
        omom_step = sem("omom_step")
        ostat_done = sem("ostat_done")
        olog_done = sem("olog_done")
        orstd_done = sem("orstd_done")
        y_done = sem("y_done")
        y_step = sem("y_step")
        scored = sem("scored")
        res_done = sem("res_done")
        row_copy = sem("row_copy")
        slot_copy = sem("slot_copy")
        xf_done = sem("xf_done")
        sel_done = sem("sel_done")
        xT_full = sem("xT_full")
        xT_done = sem("xT_done")
        h_full = sem("h_full")
        h_done = sem("h_done")
        hT_full = sem("hT_full")
        hT_done = sem("hT_done")
        yx_full = sem("yx_full")
        yx_done = sem("yx_done")
        x_in = [sem(f"x_in{c}") for c in range(4)]
        row_out = [sem(f"row_out{q}") for q in range(4)]
        xs_in = [sem(f"xs_in{q}") for q in range(NS)]
        y_out = [sem(f"y_out{q}") for q in range(NS)]
        got_in = [sem(f"got_in{q}") for q in range(4)]
        base_in, base_out = [base_in0, base_in1], [base_out0, base_out1]

        x_dram = a["x"].rearrange("(n p) d -> p n d", p=P)
        out_dram = out.rearrange("(n p) d -> p n d", p=P)
        rows_dram = nc.dram_tensor("rows_by_slot", (ST * P, XW), F32, kind="Internal").ap()
        y_dram = nc.dram_tensor("y_by_slot", (ST * P, D), F32, kind="Internal").ap()
        rows_tiles = rows_dram.rearrange("(n p) d -> p n d", p=P)
        y_tiles = y_dram.rearrange("(n p) d -> p n d", p=P)
        XC = NT // 4

        block = ctx.enter_context(nc.Block())

        W_IN = 13 * 16

        @block.sync
        def _(sp):
            def chunk(c):
                sp.dma_start(xn_all[:, c * XC:(c + 1) * XC, 0:D], x_dram[:, c * XC:(c + 1) * XC, :]).then_inc(x_in[c], 16)

            def flat(t):
                names = " ".join("abcd"[:len(t.shape) - 1])
                return t[:] if len(t.shape) == 2 else t[:].rearrange(f"p {names} -> p ({names})")

            chunk(0)
            chunk(1)
            for dst, name in ((ident, "c_ident"), (gate, "gate"), (rmsw, "rmsw")):
                sp.dma_start(dst[:], a[name]).then_inc(gate_in, 16)
            sp.dma_start(wstage[:], a["w4"].rearrange("k p d -> p k d")).then_inc(wstage_in, 16)
            for dst, name in ((wlog, "wlog"), (zbias, "zbias")):
                sp.dma_start(dst[:], a[name]).then_inc(wlog_in, 16)
            chunk(2)
            chunk(3)
            for dst, name in ((prow, "c_prow"), (bias32, "bias"), (eid, "c_eid"), (kP, "c_kP"), (tileid, "c_tile"), (own, "c_own"),
                              (lng, "lng"), (lnb, "lnb")):
                sp.dma_start(dst[:], a[name]).then_inc(w_in, 16)
            for dst, name in ((before, "c_before"), (allones, "c_all"), (level, "c_level"), (rep, "c_rep")):
                sp.dma_start(flat(dst), a[name].bitcast(BF16)).then_inc(w_in, 16)
            sp.dma_start(val[VR:KR].rearrange("p h t -> p (h t)"), a["c_causal"].bitcast(BF16)).then_inc(w_in, 16)
            sp.dma_start(flat(w2), a["w2"]).then_inc(w2_in, 16)

            def load_base(b, k, half):
                for n in range(2):
                    if half and n == 1:
                        sp.dma_start(base[:, k, 2:4, :], out_dram[:, bass.ds(2 * b - NB, 2), :]).then_inc(base_in[k], 16)
                    elif half:
                        sp.dma_start(base[:, k, 0:2, :], x_dram[:, bass.ds(2 * b, 2), :]).then_inc(base_in[k], 16)
                    else:
                        sp.dma_start(base[:, k, n:n + 1, :], x_dram[:, bass.ds(2 * b + n, 1), :]).then_inc(base_in[k], 16)

            def store(b, i, k, half):
                if half:
                    sp.wait_ge(res_done, 2 * b - (NB - 2))
                    sp.dma_start(out_dram[:, bass.ds(2 * b, 2), :], base[:, k, 0:2, :]).then_inc(base_out[k], 16)
                    sp.dma_start(out_dram[:, bass.ds(2 * b - NB, 2), :], base[:, k, 2:4, :]).then_inc(base_out[k], 16)
                else:
                    sp.wait_ge(y_step, 3 * b + 3)
                    for n in range(2):
                        sp.dma_start(out_dram[:, bass.ds(2 * b + n, 1), :], base[:, k, n:n + 1, :]).then_inc(base_out[k], 16)
                sp.wait_ge(base_out[k], 32 * i + 32)

            def value_rows(c):
                for p in range(NP3):
                    sp.wait_ge(part_step, 5 * c + (2, 4, 5)[p])
                    for g in range(2):
                        n = HG * LV
                        sp.dma_start(vparts[p * n:(p + 1) * n, g, :], p3[g * n:(g + 1) * n, p, :]).then_inc(vrows, 16)

            load_base(0, 0, False)
            load_base(1, 1, False)
            sp.wait_ge(mn_full, 4)
            sp.dma_start(flat(wstage), a["w1"]).then_inc(w1_in, 16)
            sp.wait_ge(zero_set, 1)
            sp.dma_start(rows_tiles, rowst[:, 0:1, :].broadcast_to([P, ST, XW])).then_inc(zeroed, 16)
            value_rows(0)

            def body(b, i, k, stored_half, loaded_half):
                value_rows(b + 1)
                store(b - 1, i - (1 - k), 1 - k, stored_half)
                load_base(b + 1, 1 - k, loaded_half)

            value_rows(1)
            body(1, 0, 1, False, False)
            with sp.Fori(1, HALF // 2 - 1) as i:
                body(2 * i, i, 0, False, False)
                body(2 * i + 1, i, 1, False, False)
            body(HALF - 2, HALF // 2 - 1, 0, False, False)
            body(HALF - 1, HALF // 2 - 1, 1, False, True)

            for q in range(4):
                sp.wait_ge(row_out[q], 16 * HALF)
            sp.wait_ge(av_done, 3 * HALF)
            for q in range(NS):
                sp.dma_start(xs[:, q, :], rows_tiles[:, q, :]).then_inc(xs_in[q], 16)
            for q in range(NS):
                sp.wait_ge(xf_done, q + 1)
                sp.dma_start(xs[:, q, :], rows_tiles[:, NS + q, :]).then_inc(xs_in[q], 16)

            def exchange(k, q, last):
                sp.wait_ge(yx_done, k + 1)
                sp.dma_start(y_tiles[:, bass.ds(k, 1), :], yb[:, q:q + 1, :]).then_inc(y_out[q], 16)
                if not last:
                    sp.wait_ge(xf_done, k + (NS + 1))
                    sp.dma_start(xs[:, q:q + 1, :], rows_tiles[:, bass.ds(k + 2 * NS, 1), :]).then_inc(xs_in[q], 16)

            with sp.Fori(0, ST // NS - 2) as i:
                for q in range(NS):
                    exchange(NS * i + q, q, False)
            for k in range(ST - 2 * NS, ST):
                exchange(k, k % NS, True)

            body(HALF, HALF // 2, 0, False, True)
            body(HALF + 1, HALF // 2, 1, True, True)
            with sp.Fori(HALF // 2 + 1, NB // 2 - 1) as i:
                body(2 * i, i, 0, True, True)
                body(2 * i + 1, i, 1, True, True)
            body(NB - 2, NB // 2 - 1, 0, True, True)
            store(NB - 2, NB // 2 - 1, 0, True)
            store(NB - 1, NB // 2 - 1, 1, True)

        @block.tensor
        def _(pe):
            def three_passes(dst, lhs, rhs):
                nc.tensor.matmul(dst, lhs(0), rhs(0), start=True, stop=False)
                nc.tensor.matmul(dst, lhs(0), rhs(1), start=False, stop=False)
                return nc.tensor.matmul(dst, lhs(1), rhs(0), start=False, stop=True)

            def mn_products():
                pe.wait_ge(wstage_in, 16)
                for k in range(4):
                    src = 2 * (k // 2)
                    for q in range(4):
                        h = 4 * (k % 2) + q
                        dst = (sc[:, k % 2] if k < 2 else misc[:, k - 1, :].rearrange("p (h d) -> p h d", d=D))[:, q]
                        mm = nc.tensor.matmul(dst, wstage[:, src, h * D:(h + 1) * D], wstage[:, src + 1, h * D:(h + 1) * D],
                                              start=True, stop=True)
                    mm.then_inc(mn_full, 1)

            def router(c):
                groups = range(c * NG // 4, (c + 1) * NG // 4)
                pe.wait_ge(xn_done, c + 1)
                for j in groups:
                    for n in range(GRP):
                        mm = nc.tensor.transpose(arg_bank[j % 2][:, n * P:(n + 1) * P], xn_all[:, j * GRP + n, 0:D], ident[:])
                    mm.then_inc(turned, 1)
                    if j > groups[0]:
                        logit_group(j - 1)
                logit_group(groups[-1])

            def logit_group(j):
                pe.wait_ge(unturned, j + 1)
                for n in range(GRP):
                    at = (j * GRP + n) * E
                    mm = nc.tensor.matmul(acc[:].rearrange("p a d -> p (a d)")[:, at:at + E], stageT[j % 2][:, n * P:(n + 1) * P], gate[:],
                                          start=True, stop=True, skip_group_check=True)
                mm.then_inc(logit_full, 1)

            def ranks():
                pe.wait_ge(onehot_done, 1)
                nc.tensor.matmul(arg_bank[0], before[:], onehot, start=True, stop=True)
                nc.tensor.matmul(arg_bank[1], allones[:], onehot, start=True, stop=True).then_inc(rank_full, 1)

            def free_bank(b, r):
                if not (b is None and nth(b, r) < BANKS):
                    pe.wait_ge(misc_used, nth(b, r) - (BANKS - 1))

            def r_turn(b, r, c):
                pe.wait_ge(xnb_done, c + 1)
                free_bank(b, r)
                for n in range(2):
                    mm = nc.tensor.transpose(misc[:, bank(b, r), n * P:(n + 1) * P], xnb[:, n], ident[:])
                mm.then_inc(misc_full, 1)

            def r_logits(b, r, k, turn):
                pe.wait_ge(misc_used, nth(b, turn) + 1)
                free_bank(b, r)
                for g in range(2):
                    mm = three_passes(misc[0:VC, bank(b, r), g * T:(g + 1) * T], lambda p: wlog_p[:, p, g * VC:(g + 1) * VC],
                                      lambda p: xT_p[:, k, p, :])
                mm.then_inc(misc_full, 1)

            def r_z(b, k, part):
                for n in part:
                    r = f"Z{n}"
                    free_bank(b, r)
                    for q in range(2):
                        mm = three_passes(misc[:, bank(b, r), q * T:(q + 1) * T], lambda p: m_p[:, p, 2 * n + q, :],
                                          lambda p: xT_p[:, k, p, :])
                    mm.then_inc(misc_full, 1)

            def r_u(b, k, part):
                for n in part:
                    r = f"U{n}"
                    free_bank(b, r)
                    ks, half = n // 2, n % 2
                    three_passes(misc[:, bank(b, r), :], lambda p: xT_p[:, k, p, ks * P:(ks + 1) * P],
                                 lambda p: n_p[:, p, half * 512:(half + 1) * 512]).then_inc(misc_full, 1)

            def r_gt(b, c):
                pe.wait_ge(scan_done, c + 1)
                free_bank(b, "GT")
                for n in range(2):
                    mm = nc.tensor.transpose(misc[:, bank(b, "GT"), n * VC:(n + 1) * VC], gsum[:, n * P:(n + 1) * P], ident[0:VC, 0:VC])
                mm.then_inc(misc_full, 1)

            def r_v(b, c, n):
                r = f"V{n}"
                pe.wait_ge(vrows, NP3 * 2 * 16 * c + NP3 * 2 * 16)
                free_bank(b, r)
                for q in range(2):
                    h = 2 * n + q
                    mm = nc.tensor.matmul(misc[0:VR, bank(b, r), q * T:(q + 1) * T], rep[:, h % HG, :], vparts[:, h // HG, :],
                                          start=True, stop=True)
                mm.then_inc(misc_full, 1)

            def arguments(b, k, n, first):
                ks, qt = UNITS[n]
                if n == 0:
                    pe.wait_ge(misc_used, nth(None if first else b - 1, "V3") + 1)
                if not (first and n == 0):
                    pe.wait_ge(exp_done, 3 * b + n)
                for j in range(P // TW):
                    t = qt * P + j * TW
                    w = T - TW - (t - ks * P)
                    mm = nc.tensor.matmul(arg[:, j // 16, :, (j % 16) * TW:(j % 16 + 1) * TW], level[:, w:w + P],
                                          val[:, :, t:t + TW], start=(j % 16 == 0), stop=True, skip_group_check=True)
                mm.then_inc(arg_full, 1)

            def scores(b, k, n, first, halves=(0, 1)):
                ks, qt = UNITS[n]
                for half in halves:
                    if not (first and n == 0):
                        pe.wait_ge(mult_done, 6 * b + (2 * n + half - 1))
                    if n == 0 and half == 1:
                        pe.wait_ge(misc_used, nth(None if first else b - 1, "Z3") + 1)
                    three_passes(sc[:, half], lambda p: xT_p[:, k, p, ks * P:(ks + 1) * P],
                                 lambda p: z_p[:, p, 4 * half:4 * half + 4, qt * P:(qt + 1) * P]).then_inc(s_full, 1)

            def weigh(b, n, first, heads=range(H)):
                ks, qt = UNITS[n]
                if 0 in heads:
                    if n == 0 and not first:
                        pe.wait_ge(ln_step, 4 * b - 3)
                    pe.wait_ge(mult_done, 6 * b + (2 * n + 2))
                    pe.wait_ge(misc_used, nth(b, f"U{2 * ks + 1}") + 1)
                for h in heads:
                    mm = nc.tensor.matmul(acc[:, qt, :], att[:, n, h, :], u[:, ks, h * D:(h + 1) * D],
                                          start=(h == 0 and n < 2), stop=(h == H - 1 and n != 1))
                if H - 1 in heads:
                    mm.then_inc(av_done, 1)

            def body(b, k, first=False, left=NB, seam=False):
                c, kn = b + 1, 1 - k
                rest = not (first or seam)
                one, two = left >= 1, left >= 2
                first_heads, last_heads = range(H // 2), range(H // 2, H)
                if rest:
                    weigh(b - 1, 2, False)
                arguments(b, k, 0, first)
                scores(b, k, 0, first, (0,))
                r_u(b, k, (0,))
                scores(b, k, 0, first, (1,))
                r_u(b, k, (1,))
                arguments(b, k, 1, first)
                r_u(b, k, (2, 3))
                scores(b, k, 1, first, (0,))
                if one:
                    r_gt(b, c)
                scores(b, k, 1, first, (1,))
                arguments(b, k, 2, first)
                weigh(b, 0, first, first_heads)
                scores(b, k, 2, first)
                if two:
                    r_turn(b, "T", b + 2)
                if one:
                    r_z(b, kn, (0, 1))
                if two:
                    r_logits(b, "DL", k, "T")
                if one:
                    r_z(b, kn, (2, 3))
                weigh(b, 0, first, last_heads)
                weigh(b, 1, first, first_heads)
                if one:
                    for n in range(3):
                        r_v(b, c, n)
                weigh(b, 1, first, last_heads)
                if one:
                    r_v(b, c, 3)

            def experts():
                def expert_of(n, k):
                    return nc.tensor.value_load(texpi[0:1, bass.ds(k, 1)], min_val=0, max_val=E - 1)

                def turn_rows(k, q):
                    pe.wait_ge(xf_done, k + 1)
                    nc.tensor.transpose(sc[:, q % 2, 0, :], xf[:, q % 2, :], ident[:]).then_inc(xT_full, 1)

                def hidden(k, q):
                    e = expert_of(0, k)
                    pe.wait_ge(xT_done, k + 1)
                    pe.wait_ge(sel_done, k + 1)
                    nc.tensor.matmul(arg_bank[q % 2], sel[:, q, :], bparts[:, 0:F], start=True, stop=False)
                    nc.tensor.matmul(arg_bank[q % 2], xfT[:, q % 2, :], w1[:, bass.ds(e, 1), :].rearrange("p a f -> p (a f)"),
                                     start=False, stop=True).then_inc(h_full, 1)

                def turn_hidden(k, q):
                    pe.wait_ge(h_done, k + 1)
                    for t in range(FT):
                        mm = nc.tensor.transpose(misc[:, q % 2, t * P:(t + 1) * P], hb[:, q % 2, t * P:(t + 1) * P], ident[:])
                    mm.then_inc(hT_full, 1)

                def project(k, q):
                    e = expert_of(1, k)
                    pe.wait_ge(hT_done, k + 1)
                    if not (isinstance(k, int) and k < 2):
                        pe.wait_ge(yx_done, k - 1)
                    nc.tensor.matmul(ybank[q % 2], sel[:, q, :], bparts[:, F:F + D], start=True, stop=False)
                    for t in range(FT):
                        mm = nc.tensor.matmul(ybank[q % 2], hT[:, q % 2, t * P:(t + 1) * P],
                                              w2[:, bass.ds(e, 1), t, :].rearrange("p a d -> p (a d)"), start=False, stop=(t == FT - 1))
                    mm.then_inc(yx_full, 1)

                weigh(HALF - 1, 2, False)
                pe.wait_ge(w2_in, 16)
                pe.wait_ge(w1_ready, 1)
                pe.wait_ge(misc_used, nth(HALF - 1, "V3") + 1)
                pe.wait_ge(mult_done, 6 * HALF)
                staggered(((2, turn_rows), (1, hidden), (0, turn_hidden), (-1, project)), pe)
                pe.wait_ge(yx_done, ST)

            mn_products()
            pe.wait_ge(gate_in, 48)
            pe.wait_ge(gate_ready, 1)
            router(0)
            router(1)
            pe.wait_ge(mn_used, 4)
            r_turn(None, "T0", 0)
            r_logits(None, "DL0", 0, "T0")
            r_z(None, 0, range(4))
            router(2)
            r_turn(None, "T1", 1)
            r_gt(None, 0)
            router(3)
            pe.wait_ge(w_in, W_IN)
            for n in range(3):
                r_v(None, 0, n)
            ranks()
            r_v(None, 0, 3)
            r_logits(None, "DL1", 1, "T1")
            pe.wait_ge(sorted_, 1)
            body(0, 0, first=True)
            body(1, 1)
            with pe.Fori(1, HALF // 2) as i:
                body(2 * i, 0)
                body(2 * i + 1, 1)
            experts()
            body(HALF, 0, seam=True)
            body(HALF + 1, 1)
            with pe.Fori(HALF // 2 + 1, NB // 2 - 1) as i:
                body(2 * i, 0)
                body(2 * i + 1, 1)
            body(NB - 2, 0, left=1)
            body(NB - 1, 1, left=0)
            weigh(NB - 1, 2, False)

        @block.scalar
        def _(act):
            nc.scalar.preload_act_table_set("natural_log_exp_and_others")
            act.wait_ge(const_set, CONSTS)

            def high(b, r, dst, src):
                act.wait_ge(misc_full, nth(b, r) + 1)
                nc.scalar.copy(dst, src).then_inc(high_done, 1)

            def square(c):
                act.wait_ge(chunk_step, 3 * c + 3)
                if c:
                    act.wait_ge(ssq_done, c)
                nc.scalar.activation(squares, xn_all[:, c * XC:(c + 1) * XC, 0:D], ACT.Square).then_inc(sq_done, 1)

            def spread(c):
                act.wait_ge(ssq_done, c + 1)
                t = slice(c * XC, (c + 1) * XC)
                nc.scalar.activation(lnv[:, t], dev[:, t], ACT.Ln, bias=consts[:, 0:1], scale=1.0 / D).then_inc(rstd_step, 1)
                act.wait_ge(rstd_step, c + 1)
                nc.scalar.activation(rstd[:, t], lnv[:, t], ACT.Exp, scale=-0.5).then_inc(rstd_done, 1)

            def turned_out(c, part=range(NG // 4)):
                for j in (c * NG // 4 + n for n in part):
                    act.wait_ge(turned, j + 1)
                    if j >= 2:
                        act.wait_ge(logit_full, j - 1)
                    nc.scalar.copy(stageT[j % 2], arg_bank[j % 2]).then_inc(unturned, 1)

            def turn(b, r, k):
                high(b, r, xT_p[:, k, 0, :], misc[:, bank(b, r), 0:T])

            def logits(b, r):
                act.wait_ge(misc_full, nth(b, r) + 1)
                for g in range(2):
                    nc.scalar.activation(zz[:, g, :], misc[0:VC, bank(b, r), g * T:(g + 1) * T], ACT.Identity,
                                         bias=zbias[:, g:g + 1]).then_inc(zz_done, 1)

            def softlog(b, r, c):
                act.wait_ge(misc_used, nth(b, r) + 1)
                nc.scalar.activation(na[:], na[:], ACT.Exp).then_inc(ex_done, 1)
                act.wait_ge(ex_done, c + 1)
                nc.scalar.activation(na[:], na[:], ACT.Ln, bias=consts[0:VC, 1:2]).then_inc(l1_done, 1)

            def loglam(c):
                act.wait_ge(sp_done, c + 1)
                nc.scalar.activation(lnlam[:], zz[:, 0, :], ACT.Ln, bias=consts[0:VC, 2:3]).then_inc(lnlam_done, 1)

            def z_out(b, part):
                for n in part:
                    high(b, f"Z{n}", z_p[:, 0, 2 * n:2 * n + 2, :], misc[:, bank(b, f"Z{n}"), :].rearrange("p (h t) -> p h t", h=2))

            def exps(b, k, n, first):
                ks, qt = UNITS[n]
                m = (3 * k + n) % 2
                act.wait_ge(arg_full, 3 * b + (n + 1))
                if not (first and n < 2):
                    act.wait_ge(mult_done, 6 * b + (2 * n - 2))
                for h in range(H):
                    ins = nc.scalar.activation(expo[:, m, h, :].rearrange("p (a c) -> p a c", a=2), arg[:, :, h, :], ACT.Exp,
                                               bias=negG[:, k, ks, h:h + 1])
                ins.then_inc(exp_done, 1)

            def out_rstd(b):
                act.wait_ge(ostat_done, b + 1)
                nc.scalar.activation(orstd[:], odev[:], ACT.Ln, bias=consts[:, 0:1], scale=1.0 / D).then_inc(olog_done, 1)
                act.wait_ge(olog_done, b + 1)
                nc.scalar.activation(orstd[:], orstd[:], ACT.Exp, scale=-0.5).then_inc(orstd_done, 1)

            def body(b, k, first=False, left=NB):
                c, kn = b + 1, 1 - k
                one, two = left >= 1, left >= 2
                if one:
                    softlog(None if first else b - 1, "DL1" if first else "DL", c)
                exps(b, k, 0, first)
                if one:
                    loglam(c)
                if not first:
                    out_rstd(b - 1)
                exps(b, k, 1, first)
                exps(b, k, 2, first)
                if two:
                    turn(b, "T", k)
                if one:
                    z_out(b, (0, 1))
                if two:
                    logits(b, "DL")
                if one:
                    z_out(b, (2, 3))

            def experts():
                def rows_turned(k, q):
                    act.wait_ge(xT_full, k + 1)
                    if not (isinstance(k, int) and k < 2):
                        act.wait_ge(h_full, k - 1)
                    nc.scalar.copy(xfT[:, q % 2, :], sc[:, q % 2, 0, :]).then_inc(xT_done, 1)

                def silu(k, q):
                    act.wait_ge(h_full, k + 1)
                    if not (isinstance(k, int) and k < 2):
                        act.wait_ge(hT_full, k - 1)
                    nc.scalar.activation(hb[:, q % 2, :], arg_bank[q % 2], ACT.Silu).then_inc(h_done, 1)

                nc.scalar.preload_act_table_set("silu_and_others")
                staggered(((2, rows_turned), (1, silu)), act)
                nc.scalar.preload_act_table_set("natural_log_exp_and_others")

            square(0)
            spread(0)
            square(1)
            spread(1)
            for k in range(2):
                act.wait_ge(mn_full, 3 + k)
                nc.scalar.copy(n_p[:, 0, 512 * k:512 * k + 512], misc[:, 1 + k, :]).then_inc(n_high, 1)
            turned_out(0)
            square(2)
            turned_out(1)
            spread(2)
            turn(None, "T0", 0)
            act.wait_ge(wlog_in, 32)
            logits(None, "DL0")
            z_out(None, range(4))
            square(3)
            softlog(None, "DL0", 0)
            turned_out(2, range(2))
            spread(3)
            turned_out(2, range(2, 4))
            turn(None, "T1", 1)
            loglam(0)
            turned_out(3)
            act.wait_ge(rr_step, 2)
            nc.scalar.activation(lnv[:], msq[:], ACT.Ln, bias=consts[:, 3:4], scale=1.0 / D).then_inc(rr_step, 1)
            act.wait_ge(rr_step, 3)
            nc.scalar.activation(xn_all[:, :, C_RMS], lnv[:], ACT.Exp, scale=-0.5).then_inc(rr_done, 1)
            act.wait_ge(sort_step, 4)
            nc.scalar.activation(grid[1], grid[1], ACT.Exp).then_inc(score_exp, 1)
            logits(None, "DL1")
            act.wait_ge(sorted_, 1)
            body(0, 0, first=True)
            body(1, 1)
            with act.Fori(1, HALF // 2) as i:
                body(2 * i, 0)
                body(2 * i + 1, 1)
            experts()
            with act.Fori(HALF // 2, NB // 2 - 1) as i:
                body(2 * i, 0)
                body(2 * i + 1, 1)
            body(NB - 2, 0, left=1)
            body(NB - 1, 1, left=0)
            out_rstd(NB - 1)

        def as_f32(ap):
            return ap.bitcast(F32)

        @block.vector
        def _(dve):
            nc.vector.memset(rowst[:, 0, :], 0.0).then_inc(zero_set, 1)
            fills = [(consts[:, 0:1], 1e-5), (consts[:, 1:2], 1.0), (consts[:, 2:3], LAM_MIN), (consts[:, 3:4], 1e-6), (ones[:], 1.0),
                     (ones128[:], 1.0), (idle0[:], 0.0), (xn_all[:, :, D:XW], 0.0)]
            assert len(fills) == CONSTS
            for dst, v in fills:
                nc.vector.memset(dst, v).then_inc(const_set, 1)

            def col(t, c):
                return t[:, c * XC:(c + 1) * XC].rearrange("p (t a) -> p t a", a=1).broadcast_to([P, XC, D])

            def centre(c):
                xc = xn_all[:, c * XC:(c + 1) * XC, 0:D]
                t = slice(c * XC, (c + 1) * XC)
                dve.wait_ge(x_in[c], 16)
                nc.vector.tensor_reduce(ssum[:, t], xc, AX_X, ALU.add).then_inc(chunk_step, 1)
                dve.wait_ge(chunk_step, 3 * c + 1)
                nc.vector.tensor_scalar(mean[:, t], ssum[:, t], 1.0 / D, None, ALU.mult).then_inc(chunk_step, 1)
                dve.wait_ge(chunk_step, 3 * c + 2)
                nc.vector.tensor_tensor(xc, xc, col(mean, c), ALU.subtract).then_inc(chunk_step, 1)

            def deviation(c):
                dve.wait_ge(sq_done, c + 1)
                nc.vector.tensor_reduce(dev[:, c * XC:(c + 1) * XC], squares.rearrange("p (t d) -> p t d", d=D), AX_X,
                                        ALU.add).then_inc(ssq_done, 1)

            def scale(c):
                xc = xn_all[:, c * XC:(c + 1) * XC, 0:D]
                dve.wait_ge(rstd_done, c + 1)
                nc.vector.tensor_tensor(xc, xc, col(rstd, c), ALU.mult).then_inc(xn_done, 1)

            def split_weights():
                dve.wait_ge(wlog_in, 32)
                nc.vector.tensor_copy(wlog_p[:, 0, :], wlog[:]).then_inc(wlog_step, 1)
                dve.wait_ge(wlog_step, 1)
                nc.vector.tensor_tensor(wlog_p[:, 1, :], wlog[:], as_f32(wlog_p[:, 0, :]), ALU.subtract).then_inc(wlog_step, 1)
                for k in range(2):
                    dve.wait_ge(mn_full, 1 + k)
                    hi, lo = m_p[:, 0, 4 * k:4 * k + 4, :], m_p[:, 1, 4 * k:4 * k + 4, :]
                    nc.vector.tensor_scalar(hi, sc[:, k], float(D) ** -0.5, None, ALU.mult).then_inc(mn_step, 1)
                    dve.wait_ge(mn_step, k + 1)
                    nc.vector.scalar_tensor_tensor(out=lo, in0=sc[:, k], scalar=float(D) ** -0.5, in1=as_f32(hi), op0=ALU.mult,
                                                   op1=ALU.subtract).then_inc(mn_used, 1)
                for k in range(2):
                    dve.wait_ge(n_high, k + 1)
                    at = slice(512 * k, 512 * k + 512)
                    nc.vector.tensor_tensor(n_p[:, 1, at], misc[:, 1 + k, :], as_f32(n_p[:, 0, at]), ALU.subtract).then_inc(mn_used, 1)

            def low(b, r, dst, src, hi):
                dve.wait_ge(high_done, nth_cut(b, r) + 1)
                nc.vector.tensor_tensor(dst, src, as_f32(hi), ALU.subtract).then_inc(misc_used, 1)

            def turn(b, r, k):
                low(b, r, xT_p[:, k, 1, :], misc[:, bank(b, r), 0:T], xT_p[:, k, 0, :])

            def z_out(b, part):
                for n in part:
                    low(b, f"Z{n}", z_p[:, 1, 2 * n:2 * n + 2, :], misc[:, bank(b, f"Z{n}"), :].rearrange("p (h t) -> p h t", h=2),
                        z_p[:, 0, 2 * n:2 * n + 2, :])

            def u_out(b, part):
                for n in part:
                    dve.wait_ge(misc_full, nth(b, f"U{n}") + 1)
                    nc.vector.tensor_copy(u[:, n // 2, (n % 2) * 512:(n % 2 + 1) * 512], misc[:, bank(b, f"U{n}"), :]).then_inc(misc_used, 1)

            def minus_abs(c):
                dve.wait_ge(zz_done, 2 * c + 2)
                nc.vector.scalar_tensor_tensor(out=na[:], in0=zz[:], scalar=-1.0, in1=zz[:], op0=ALU.mult, op1=ALU.min).then_inc(misc_used, 1)

            def softplus_scan(c):
                dve.wait_ge(l1_done, c + 1)
                nc.vector.scalar_tensor_tensor(out=zz[:], in0=zz[:], scalar=0.0, in1=na[:], op0=ALU.max, op1=ALU.add).then_inc(sp_done, 1)
                dve.wait_ge(sp_done, c + 1)
                nc.vector.tensor_tensor_scan(gsum[:], ones[:], zz[:, 1, :], 0.0, ALU.mult, ALU.subtract).then_inc(scan_done, 1)

            def parts(c, first=False):
                dve.wait_ge(lnlam_done, c + 1)
                dve.wait_ge(scan_done, c + 1)
                nc.vector.tensor_tensor(v32[:], lnlam[:], gsum[:], ALU.add).then_inc(part_step, 1)
                if not first:
                    dve.wait_ge(vrows, NP3 * 2 * 16 * c)
                dve.wait_ge(part_step, 5 * c + 1)
                nc.vector.tensor_copy(p3[:, 0, :], v32[:]).then_inc(part_step, 1)
                dve.wait_ge(part_step, 5 * c + 2)
                nc.vector.tensor_tensor(v32[:], v32[:], p3[:, 0, :], ALU.subtract).then_inc(part_step, 1)
                dve.wait_ge(part_step, 5 * c + 3)
                nc.vector.tensor_copy(p3[:, 1, :], v32[:]).then_inc(part_step, 1)
                dve.wait_ge(part_step, 5 * c + 4)
                nc.vector.tensor_tensor(p3[:, 2, :], v32[:], p3[:, 1, :], ALU.subtract).then_inc(part_step, 1)

            def gates_out(b, k):
                dve.wait_ge(misc_full, nth(b, "GT") + 1)
                src = misc[:, bank(b, "GT"), 0:2 * VC].rearrange("p (a h l) -> p a h l", a=2, l=LV)[:, :, :, 0]
                nc.vector.tensor_scalar(negG[:, k], src, -1.0, None, ALU.mult).then_inc(misc_used, 1)

            def values_out(b, part=range(4)):
                for n in part:
                    r = f"V{n}"
                    dve.wait_ge(misc_full, nth(b, r) + 1)
                    nc.vector.tensor_tensor(val[0:VR, 2 * n:2 * n + 2, :], misc[0:VR, bank(b, r), :].rearrange("p (h t) -> p h t", h=2),
                                            own[:].rearrange("p (a t) -> p a t", a=1).broadcast_to([VR, 2, T]), ALU.mult).then_inc(misc_used, 1)

            def products(b, k, n, first, halves=(0, 1)):
                m = (3 * k + n) % 2
                if 0 in halves:
                    dve.wait_ge(exp_done, 3 * b + (n + 1))
                    if not first:
                        dve.wait_ge(av_done, 3 * b + (n - 2))
                for half in halves:
                    dve.wait_ge(s_full, 6 * b + (2 * n + half + 1))
                    nc.vector.tensor_tensor(att[:, n, 4 * half:4 * half + 4, :], sc[:, half], expo[:, m, 4 * half:4 * half + 4, :],
                                            ALU.mult).then_inc(mult_done, 1)

            def moments(st, total, diff, mu, dv, done, c):
                nc.vector.tensor_tensor(diff[:], st[:, :, 1], st[:, :, 4], ALU.subtract).then_inc(done, 1)
                nc.vector.tensor_tensor(total[:], st[:, :, 1:3], st[:, :, 4:6], ALU.add).then_inc(done, 1)
                dve.wait_ge(done, c + 2)
                nc.vector.tensor_tensor(diff[:], diff[:], diff[:], ALU.mult).then_inc(done, 1)
                nc.vector.tensor_scalar(mu[:], total[:, :, 0], 0.5, None, ALU.mult).then_inc(done, 1)
                dve.wait_ge(done, c + 4)
                return nc.vector.scalar_tensor_tensor(out=dv[:], in0=diff[:], scalar=D / 4.0, in1=total[:, :, 1], op0=ALU.mult, op1=ALU.add)

            def statistics(b):
                dve.wait_ge(av_done, 3 * b + 3)
                nc.vector.tensor_tensor(o[:], acc[:, 0:2, :], xn_all[:, bass.ds(2 * b, 2), 0:D], ALU.add).then_inc(ln_step, 1)
                dve.wait_ge(ln_step, 4 * b + 1)
                for n in range(2):
                    nc.vector.bn_stats(ostats[:, n, :], o[:, n, :]).then_inc(ln_step, 1)
                dve.wait_ge(ln_step, 4 * b + 3)
                moments(ostats, osum, odif, omean, odev, omom_step, 4 * b).then_inc(ostat_done, 1)

            def normalise(b):
                if not (isinstance(b, int) and b == 0):
                    dve.wait_ge(y_step, 3 * b)
                dve.wait_ge(orstd_done, b + 1)
                nc.vector.tensor_scalar(y[:, 0, :], o[:, 0, :], omean[:, 0:1], orstd[:, 0:1], ALU.subtract, ALU.mult).then_inc(ln_step, 1)
                nc.vector.tensor_scalar(y[:, 1, :], o[:, 1, :], omean[:, 1:2], orstd[:, 1:2], ALU.subtract, ALU.mult).then_inc(y_done, 1)

            def body(b, k, first=False, left=NB):
                c, kn = b + 1, 1 - k
                one, two = left >= 1, left >= 2
                if one:
                    softplus_scan(c)
                if not first:
                    statistics(b - 1)
                u_out(b, (0, 1))
                products(b, k, 0, first)
                if not first:
                    normalise(b - 1)
                u_out(b, (2,))
                products(b, k, 1, first, (0,))
                u_out(b, (3,))
                products(b, k, 1, first, (1,))
                if one:
                    parts(c)
                    gates_out(b, kn)
                if two:
                    turn(b, "T", k)
                if one:
                    z_out(b, (0, 1))
                products(b, k, 2, first, (0,))
                if two:
                    minus_abs(b + 2)
                if one:
                    z_out(b, (2, 3))
                products(b, k, 2, first, (1,))
                if one:
                    values_out(b)

            def sort():
                count = [0]

                def then(ins):
                    count[0] += 1
                    ins.then_inc(sort_step, 1)
                    dve.wait_ge(sort_step, count[0])

                def te(x):
                    return x.rearrange("p (t e) -> p t e", e=E)

                def over_e(col):
                    return col.rearrange("p (t a) -> p t a", a=1).broadcast_to([P, NT, E])

                def over_t(row, n=NT):
                    return row.rearrange("p (a e) -> p a e", a=1).broadcast_to([P, n, E])

                logit, gap, low, oh, pos, carry = grid[0], grid[1], grid[2], grid[3], grid[4], grid[5]
                top, expert = small64[:, 0, :], small64[:, 1, :]
                total, tiles, ends, starts = small[:, 0], small[:, 1], small[:, 2], small[:, 3]
                dve.wait_ge(logit_full, NG)
                dve.wait_ge(rr_done, 1)
                rms = xn_all[:, :, C_RMS:C_RMS + 1].broadcast_to([P, NT, E])
                then(nc.vector.tensor_tensor(te(logit), te(acc[:].rearrange("p a d -> p (a d)")), rms, ALU.mult))
                then(nc.vector.tensor_reduce(top, te(logit), AX_X, ALU.max))
                then(nc.vector.tensor_tensor(te(gap), te(logit), over_e(top), ALU.subtract))
                then(nc.vector.tensor_scalar(low, gap, 0.0, float(E), ALU.is_lt, ALU.mult))
                then(nc.vector.tensor_tensor(te(low), te(low), over_t(eid[:]), ALU.add))
                then(nc.vector.tensor_reduce(expert, te(low), AX_X, ALU.min))
                then(nc.vector.tensor_tensor(te(oh), over_t(eid[:]), over_e(expert), ALU.is_equal))
                nc.vector.tensor_copy(onehot, oh).then_inc(onehot_done, 1)
                dve.wait_ge(score_exp, 1)
                then(nc.vector.tensor_reduce(top, te(gap), AX_X, ALU.add))
                then(nc.vector.reciprocal(xn_all[:, :, C_SCORE], top))
                yield
                dve.wait_ge(rank_full, 1)
                then(nc.vector.tensor_copy(pos, arg_bank[1]))
                for e in range(E):
                    ins = nc.vector.tensor_tensor_scan(te(carry)[:, :, e], ones128[:, 0:NT], te(pos)[:, :, e], 0.0, ALU.mult, ALU.add)
                    if e < E - 1:
                        ins.then_inc(sort_step, 1)
                        count[0] += 1
                then(ins)
                nc.vector.tensor_copy(total, te(carry)[:, NT - 1, :]).then_inc(sort_step, 1)
                count[0] += 1
                then(nc.vector.tensor_tensor(pos, carry, pos, ALU.subtract))
                kp = kP[:].rearrange("p (a t) -> p a t", a=1).broadcast_to([P, E, NT])
                many = total.rearrange("p (e a) -> p e a", a=1).broadcast_to([P, E, NT])
                g7 = grid[7].rearrange("p (e t) -> p e t", e=E)
                then(nc.vector.tensor_tensor(g7, many, kp, ALU.is_gt))
                then(nc.vector.tensor_reduce(tiles, g7, AX_X, ALU.add))
                then(nc.vector.tensor_tensor_scan(ends, ones128[:, 0:E], tiles, 0.0, ALU.mult, ALU.add))
                then(nc.vector.tensor_tensor(starts, ends, tiles, ALU.subtract))
                then(nc.vector.tensor_scalar(starts, starts, float(P), None, ALU.mult))
                then(nc.vector.tensor_tensor(te(pos), te(pos), over_t(starts), ALU.add))
                then(nc.vector.tensor_tensor(pos, pos, arg_bank[0], ALU.add))
                then(nc.vector.tensor_tensor(pos, pos, oh, ALU.mult))
                then(nc.vector.tensor_reduce(expert, te(pos), AX_X, ALU.add))
                then(nc.vector.tensor_copy(slot[:], expert))
                tg = tgrid.rearrange("p (t e) -> p t e", e=E)
                tid = tileid[:].rearrange("p (t a) -> p t a", a=1).broadcast_to([P, ST, E])
                then(nc.vector.tensor_tensor(tg, over_t(ends, ST), tid, ALU.is_le))
                then(nc.vector.tensor_reduce(texp[:], tg, AX_X, ALU.add))
                then(nc.vector.tensor_scalar(texp[:], texp[:], float(E - 1), None, ALU.min))
                then(nc.vector.tensor_scalar(tsel[:], texp[0:NP3 * E, :], prow[:, 0:1], None, ALU.is_equal))
                nc.vector.tensor_copy(texpi[:], texp[0:1, :]).then_inc(sorted_, 1)

            def experts():
                def scale_rows(k, q):
                    dve.wait_ge(xs_in[q], 16 * ((k - q) // NS) + 16 if isinstance(k, int) else 4 * (k - q) + 16)
                    if not (isinstance(k, int) and k < 2):
                        dve.wait_ge(xT_full, k - 1)
                    nc.vector.tensor_scalar(xf[:, q % 2, :], xs[:, q, 0:D], xs[:, q, C_RMS:C_RMS + 1], None, ALU.mult).then_inc(xf_done, 1)

                def select(k, q):
                    if not (isinstance(k, int) and k < NS):
                        dve.wait_ge(yx_full, k - 3)
                    nc.vector.tensor_scalar(sel[:, q, :], ones128[0:NP3 * E, :], tsel[:, bass.ds(k, 1)], None, ALU.mult).then_inc(sel_done, 1)

                def hidden_turned(k, q):
                    dve.wait_ge(hT_full, k + 1)
                    if not (isinstance(k, int) and k < 2):
                        dve.wait_ge(yx_full, k - 1)
                    nc.vector.tensor_copy(hT[:, q % 2, :], misc[:, q % 2, :]).then_inc(hT_done, 1)

                def output(k, q):
                    dve.wait_ge(yx_full, k + 1)
                    if not (isinstance(k, int) and k < NS):
                        dve.wait_ge(y_out[q], 16 * ((k - q) // NS) if isinstance(k, int) else 4 * (k - q))
                    nc.vector.tensor_copy(yb[:, q, :], ybank[q % 2]).then_inc(yx_done, 1)

                staggered(((3, scale_rows), (2, select), (0, hidden_turned), (-1, output)), dve)

            centre(0)
            centre(1)
            deviation(0)
            scale(0)
            deviation(1)
            scale(1)
            centre(2)
            split_weights()
            deviation(2)
            scale(2)
            turn(None, "T0", 0)
            centre(3)
            minus_abs(0)
            z_out(None, range(4))
            deviation(3)
            scale(3)
            softplus_scan(0)
            turn(None, "T1", 1)
            parts(0, True)
            gates_out(None, 0)
            nc.vector.tensor_tensor(msq[:], dev[:], rstd[:], ALU.mult).then_inc(rr_step, 1)
            dve.wait_ge(rr_step, 1)
            nc.vector.tensor_tensor(msq[:], msq[:], rstd[:], ALU.mult).then_inc(rr_step, 1)
            dve.wait_ge(w_in, W_IN)
            sorting = sort()
            next(sorting)
            values_out(None)
            for _ in sorting:
                pass
            minus_abs(1)
            body(0, 0, first=True)
            body(1, 1)
            with dve.Fori(1, HALF // 2) as i:
                body(2 * i, 0)
                body(2 * i + 1, 1)
            experts()
            with dve.Fori(HALF // 2, NB // 2 - 1) as i:
                body(2 * i, 0)
                body(2 * i + 1, 1)
            body(NB - 2, 0, left=1)
            body(NB - 1, 1, left=0)
            statistics(NB - 1)
            normalise(NB - 1)

        @block.gpsimd
        def _(pool):
            def pair(t):
                return t[:].rearrange("p (a d) -> p a d", a=1).broadcast_to([P, 2, D])

            def stage_x(b):
                nc.gpsimd.tensor_copy(xnb[:], xn_all[:, bass.ds(2 * b, 2), 0:D]).then_inc(xnb_done, 1)

            def carry_wait():
                nc.gpsimd.tensor_tensor(idle[:], idle0[:], idle0[:], ALU.add)

            def send_rows(b, first):
                if not first:
                    for q in range(4):
                        pool.wait_ge(row_out[q], 16 * b)
                nc.gpsimd.tensor_copy(slotst[:], slot[:, bass.ds(4 * b, 4)]).then_inc(row_copy, 1)
                nc.gpsimd.tensor_copy(rowst[:], xn_all[:, bass.ds(4 * b, 4), :]).then_inc(row_copy, 1)
                pool.wait_ge(row_copy, 2 * b + 2)
                carry_wait()
                for q in range(4):
                    nc.gpsimd.indirect_dma_start(out=rows_dram, out_offset=bass.IndirectOffsetOnAxis(ap=slotst[:, q:q + 1], axis=0),
                                                 in_=rowst[:, q, :], in_offset=None).then_inc(row_out[q], 16)

            def fetch_rows(b):
                if not (isinstance(b, int) and b == HALF):
                    pool.wait_ge(res_done, 2 * b - NB)
                nc.gpsimd.tensor_copy(slotst[:, 0:2], slot[:, bass.ds(2 * b, 2)]).then_inc(slot_copy, 1)
                nc.gpsimd.tensor_copy(slotst[:, 2:4], slot[:, bass.ds(2 * b - NB, 2)]).then_inc(slot_copy, 1)
                pool.wait_ge(slot_copy, 2 * b - (NB - 2))
                carry_wait()
                for q in range(4):
                    nc.gpsimd.indirect_dma_start(out=got[:, q, :], out_offset=None, in_=y_dram,
                                                 in_offset=bass.IndirectOffsetOnAxis(ap=slotst[:, q:q + 1], axis=0)).then_inc(got_in[q], 16)

            def finish(b, i, k, half):
                pool.wait_ge(y_done, b + 1)
                pool.wait_ge(ln_step, 4 * b + 4)
                nc.gpsimd.tensor_tensor(y[:], y[:], pair(lng), ALU.mult).then_inc(y_step, 1)
                pool.wait_ge(y_step, 3 * b + 1)
                nc.gpsimd.tensor_tensor(y[:], y[:], pair(lnb), ALU.add).then_inc(y_step, 1)
                pool.wait_ge(base_in[k], 32 * i + 32)
                pool.wait_ge(y_step, 3 * b + 2)
                nc.gpsimd.tensor_tensor(base[:, k, 0:2, :], base[:, k, 0:2, :], y[:], ALU.add).then_inc(y_step, 1)
                if half:
                    for q in range(4):
                        pool.wait_ge(got_in[q], 16 * b - 16 * (HALF - 1))
                    for n, t in ((0, 2 * b), (1, 2 * b - NB)):
                        score = xn_all[:, bass.ds(t, 2), C_SCORE:C_SCORE + 1].broadcast_to([P, 2, D])
                        nc.gpsimd.tensor_tensor(got[:, 2 * n:2 * n + 2, :], got[:, 2 * n:2 * n + 2, :], score, ALU.mult).then_inc(scored, 1)
                    pool.wait_ge(y_step, 3 * b + 3)
                    for n in range(2):
                        pool.wait_ge(scored, 2 * b - (NB - n - 1))
                        part = base[:, k, 2 * n:2 * n + 2, :]
                        nc.gpsimd.tensor_tensor(part, part, got[:, 2 * n:2 * n + 2, :], ALU.add).then_inc(res_done, 1)

            def body(b, i, k, half, first=False, more=True):
                if more:
                    pool.wait_ge(misc_full, nth(None if first else b - 1, "T1" if first else "T") + 1)
                    stage_x(b + 2)
                if half:
                    fetch_rows(b - 1)
                elif not (isinstance(b, int) and b == HALF):
                    send_rows(b, first)
                if not first:
                    finish(b - 1, i - (1 - k), 1 - k, half)

            bw = lambda c: prow[:, c:c + 1].broadcast_to([NP3 * E, F + D])
            pool.wait_ge(const_set, CONSTS)
            pool.wait_ge(gate_in, 48)
            nc.gpsimd.tensor_scalar(gate[:], gate[:], rmsw[:, 0:1], None, ALU.mult).then_inc(gate_ready, 1)
            pool.wait_ge(xn_done, 1)
            stage_x(0)
            pool.wait_ge(w_in, W_IN)
            steps = [(bparts[:], bias32[:], None), (biasr, bparts[:], 1), (bias32[:], bias32[:], biasr), (bparts[:], bias32[:], None),
                     (biasr, bparts[:], 2), (bparts[:], bias32[:], biasr)]
            for n, (dst, src, by) in enumerate(steps):
                if by is None:
                    ins = nc.gpsimd.tensor_copy(dst, src)
                elif isinstance(by, int):
                    ins = nc.gpsimd.tensor_tensor(dst, src, bw(by), ALU.mult)
                else:
                    ins = nc.gpsimd.tensor_tensor(dst, src, by, ALU.add)
                ins.then_inc(bias_step, 1)
                pool.wait_ge(bias_step, n + 1)
            pool.wait_ge(misc_full, nth(None, "T0") + 1)
            stage_x(1)
            pool.wait_ge(w1_in, 16)
            nc.gpsimd.tensor_scalar(wstage[:].rearrange("p a b -> p (a b)"), wstage[:].rearrange("p a b -> p (a b)"), rmsw[:, 0:1], None,
                                    ALU.mult).then_inc(w1_ready, 1)
            pool.wait_ge(sorted_, 1)
            pool.wait_ge(zeroed, 16)
            body(0, 0, 0, False, first=True)
            body(1, 0, 1, False)
            with pool.Fori(1, HALF // 2) as i:
                body(2 * i, i, 0, False)
                body(2 * i + 1, i, 1, False)
            for q in range(NS):
                pool.wait_ge(y_out[q], 16 * (ST // NS))
            body(HALF, HALF // 2, 0, False)
            body(HALF + 1, HALF // 2, 1, True)
            with pool.Fori(HALF // 2 + 1, NB // 2 - 1) as i:
                body(2 * i, i, 0, True)
                body(2 * i + 1, i, 1, True)
            body(NB - 2, NB // 2 - 1, 0, True, more=False)
            body(NB - 1, NB // 2 - 1, 1, True, more=False)
            fetch_rows(NB - 1)
            finish(NB - 1, NB // 2 - 1, 1, True)


NAMES = ["x", "wlog", "zbias", "lng", "lnb", "w4", "c_level", "c_own", "c_causal", "c_rep", "c_ident",
         "gate", "rmsw", "bias", "w1", "w2", "c_before", "c_all", "c_eid", "c_kP", "c_tile", "c_prow"]


def kernel(**inputs):
    import numpy as _np
    import concourse.bacc as _bacc
    from concourse import mybir as _mybir
    from concourse.bass_utils import run_bass_kernel_spmd as _run

    g = {n: _np.asarray(v) for n, v in inputs.items()}
    wdl = g["L0_attn_Wdl"].reshape(H, 12, D)[:, :LV].reshape(VC, D)
    wgr = _np.repeat(g["L0_attn_Wg"], LV, axis=0)
    lp = g["L0_attn_Lparam"][:, :LV].reshape(VC)
    bg = _np.repeat(g["L0_attn_bg"], LV)
    by_head = lambda w: w.reshape(H, D, D).transpose(1, 0, 2).reshape(D, H * D)
    data = {
        "x": g["L0_attn_x"].reshape(NB * T, D),
        "wlog": _np.concatenate([wdl, wgr]).T, "zbias": _np.stack([lp, bg], 1),
        "lng": _np.tile(g["L0_attn_ln_g"][None], (P, 1)), "lnb": _np.tile(g["L0_attn_ln_b"][None], (P, 1)),
        "w4": _np.stack([by_head(g["L0_attn_Wq"]), by_head(g["L0_attn_Wk"]), by_head(g["L0_attn_Wv"]),
                         by_head(g["L0_attn_Wo"].T)]),
        "gate": g["L0_ffn_gate_w"].T, "rmsw": g["L0_ffn_rms_w"][:, None],
        "bias": _np.tile(_np.concatenate([g["L0_ffn_b1"], g["L0_ffn_b2"]], 1), (NP3, 1)),
        "w1": g["L0_ffn_W1"].transpose(1, 0, 2).reshape(D, E * F),
        "w2": g["L0_ffn_W2"].reshape(E, FT, P, D).transpose(2, 0, 1, 3).reshape(P, E * FT * D),
        **level_constants(),
    }
    nc = _bacc.Bacc("TRN2", target_bir_lowering=False, num_devices=1)
    arrays, args = {}, {}
    for name in NAMES:
        v = _np.ascontiguousarray(data[name])
        arrays[f"in_{name}"] = v
        args[name] = nc.dram_tensor(f"in_{name}", v.shape, _mybir.dt.from_np(v.dtype), kind="ExternalInput").ap()
    out = nc.dram_tensor("out_0", (NB * T, D), _mybir.dt.from_np(_np.dtype("float32")), kind="ExternalOutput").ap()
    build(nc, args, out)
    r = _run(nc, [arrays], core_ids=[0])
    return r.results[0]["out_0"].reshape(NB, T, D)
```
